# Optimizing a Trainium2 kernel written in Bass

```python
import numpy as np
import jax
import jax.numpy as jnp

def _softmax(x, axis=-1):
    return jax.nn.softmax(x, axis=axis)

def _gelu(x):
    return jax.nn.gelu(x, approximate=True)

def _silu(x):
    return jax.nn.silu(x)

def _sigmoid(x):
    return jax.nn.sigmoid(x)

def _layernorm(x, axis=-1, eps=1e-05):
    m = jnp.mean(x, axis=axis, keepdims=True)
    v = jnp.var(x, axis=axis, keepdims=True)
    return (x - m) / jnp.sqrt(v + eps)

def _scatter_add(tgt, idx, src, axis=0):
    return tgt.at[idx].add(src)

def _segment_sum(src, seg, n):
    return jax.ops.segment_sum(src, seg, n)
kernel_name = 'mk_gnn_resnorm_d4_gnn_r64_1907f9'

def setup_inputs(seed: int=0):
    np.random.seed(seed)
    _w = jnp.asarray

    def _rec_inputs():
        import jax
        import jax.numpy as jnp
        _gk = jax.random.key(seed)
        x = -0.000202 + 1 * jax.random.normal(jax.random.fold_in(_gk, 1), (100000, 128), jnp.float32)
        src = jax.random.randint(jax.random.fold_in(_gk, 2), (25000,), 0, 100000, jnp.int32)
        dst = jax.random.randint(jax.random.fold_in(_gk, 3), (25000,), 0, 100000, jnp.int32)
        _o = jnp.argsort(dst, stable=True)
        src = src[_o]
        dst = dst[_o]
        edge_attr_128 = -5.16925e-05 + 1.00005 * jax.random.normal(jax.random.fold_in(_gk, 11), (25000, 128), jnp.float32)
        edge_weight = jax.random.uniform(jax.random.fold_in(_gk, 13), (25000,), jnp.float32, 0.0, 0.999998)
        return (x, src, dst, edge_attr_128, edge_weight)
    x, src, dst, edge_attr_128, edge_weight = _rec_inputs()

    def _L0_gnn_setup():
        import jax, jax.numpy as jnp
        import numpy as np
        N_NODES = 50000
        N_EDGES = 12500
        F_NODE = 128
        F_EDGE = 128
        HIDDEN = 128
        EPS = 1e-05

        def _glorot(key, shape):
            fan_in, fan_out = (shape[0], shape[1])
            lim = float(np.sqrt(6.0 / (fan_in + fan_out)))
            return jax.random.uniform(key, shape, jnp.float32, -lim, lim)
        key = jax.random.key(seed)
        ks = jax.random.split(key, 12)
        node_features = jax.random.normal(ks[0], (N_NODES, F_NODE), jnp.float32)
        edge_index = jax.random.randint(ks[1], (2, N_EDGES), 0, N_NODES, jnp.int64)
        edge_features = jax.random.normal(ks[2], (N_EDGES, F_EDGE), jnp.float32)
        W1 = _glorot(ks[3], (2 * F_NODE + F_EDGE, HIDDEN))
        b1 = jnp.zeros((HIDDEN,), jnp.float32)
        W2 = _glorot(ks[4], (HIDDEN, HIDDEN))
        b2 = jnp.zeros((HIDDEN,), jnp.float32)
        U1 = _glorot(ks[5], (F_NODE + HIDDEN, HIDDEN))
        ub1 = jnp.zeros((HIDDEN,), jnp.float32)
        U2 = _glorot(ks[6], (HIDDEN, F_NODE))
        ub2 = jnp.zeros((F_NODE,), jnp.float32)
        ln_w = jnp.ones((F_NODE,), jnp.float32)
        ln_b = jnp.zeros((F_NODE,), jnp.float32)
        return {'node_features': node_features, 'edge_index': edge_index, 'edge_features': edge_features, 'W1': W1, 'b1': b1, 'W2': W2, 'b2': b2, 'U1': U1, 'ub1': ub1, 'U2': U2, 'ub2': ub2, 'ln_w': ln_w, 'ln_b': ln_b}
    _L0_gnn_all = _L0_gnn_setup()
    _L0_gnn_in = {k: v for k, v in _L0_gnn_all.items() if k in ('W1', 'b1', 'W2', 'b2', 'U1', 'ub1', 'U2', 'ub2', 'ln_w', 'ln_b')}
    del _L0_gnn_all

    def _L1_gnn_setup():
        import jax, jax.numpy as jnp
        import numpy as np

        def _sage_conv(h, src, dst, num_nodes, W_l, b, W_r):
            msg = h[src]
            agg = jax.ops.segment_sum(msg, dst, num_segments=num_nodes)
            deg = jax.ops.segment_sum(jnp.ones((src.shape[0],), h.dtype), dst, num_segments=num_nodes)
            agg = agg / jnp.maximum(deg, 1.0)[:, None]
            return agg @ W_l + b + h @ W_r
        key = jax.random.key(seed)
        ks = jax.random.split(key, 8)
        N, E, D_IN, D_HID, D_OUT = (50000, 12500, 128, 128, 128)
        s = 1.0 / np.sqrt(D_IN)
        return {'x': jax.random.normal(ks[0], (N, D_IN), dtype=jnp.float32), 'edge_index': jax.random.randint(ks[1], (2, E), 0, N, dtype=jnp.int64), 'W1_l': jax.random.normal(ks[2], (D_IN, D_HID), dtype=jnp.float32) * s, 'b1': jnp.zeros((D_HID,), dtype=jnp.float32), 'W1_r': jax.random.normal(ks[3], (D_IN, D_HID), dtype=jnp.float32) * s, 'W2_l': jax.random.normal(ks[4], (D_HID, D_OUT), dtype=jnp.float32) * s, 'b2': jnp.zeros((D_OUT,), dtype=jnp.float32), 'W2_r': jax.random.normal(ks[5], (D_HID, D_OUT), dtype=jnp.float32) * s}
    _L1_gnn_all = _L1_gnn_setup()
    _L1_gnn_in = {k: v for k, v in _L1_gnn_all.items() if k in ('W1_l', 'b1', 'W1_r', 'W2_l', 'b2', 'W2_r')}
    del _L1_gnn_all

    def _L2_gnn_setup():
        import jax, jax.numpy as jnp
        import numpy as np
        N = 50000
        E = 12500
        D = 128

        def _gcn_layer(x, row, col, ew, W, b, n):
            deg = jax.ops.segment_sum(ew, col, num_segments=n)
            dis = jnp.where(deg > 0, jax.lax.rsqrt(jnp.maximum(deg, 1e-12)), 0.0)
            norm = dis[row] * ew * dis[col]
            h = x @ W
            msg = h[row] * norm[:, None]
            out = jax.ops.segment_sum(msg, col, num_segments=n)
            return out + b
        key = jax.random.key(seed)
        k1, k2, k3, k4, k5 = jax.random.split(key, 5)
        x = jax.random.normal(k1, (N, D), dtype=jnp.float32)
        edge_index = jax.random.randint(k2, (2, E), 0, N, dtype=jnp.int64)
        edge_weight = jax.random.uniform(k3, (E,), dtype=jnp.float32)
        s = 1.0 / np.sqrt(D)
        W1 = jax.random.uniform(k4, (D, D), minval=-s, maxval=s, dtype=jnp.float32)
        b1 = jnp.zeros((D,), dtype=jnp.float32)
        W2 = jax.random.uniform(k5, (D, D), minval=-s, maxval=s, dtype=jnp.float32)
        b2 = jnp.zeros((D,), dtype=jnp.float32)
        return {'x': x, 'edge_index': edge_index, 'edge_weight': edge_weight, 'W1': W1, 'b1': b1, 'W2': W2, 'b2': b2}
    _L2_gnn_all = _L2_gnn_setup()
    _L2_gnn_in = {k: v for k, v in _L2_gnn_all.items() if k in ('W1', 'b1', 'W2', 'b2')}
    del _L2_gnn_all

    def _L3_gnn_setup():
        import jax, jax.numpy as jnp
        import numpy as np
        N_NODES = 100000
        D_IN = 128
        D_OUT = 128
        N_EDGES = 25000
        BN_EPS = 1e-05

        def _glorot(key, fan_in, fan_out):
            limit = np.sqrt(6.0 / (fan_in + fan_out))
            return jax.random.uniform(key, (fan_in, fan_out), jnp.float32, -limit, limit)
        key = jax.random.key(seed)
        k_x, k_e, k0, k1, k2 = jax.random.split(key, 5)
        x = jax.random.normal(k_x, (N_NODES, D_IN), jnp.float32)
        edge_index = jax.random.randint(k_e, (2, N_EDGES), 0, N_NODES, jnp.int64)
        return {'x': x, 'edge_index': edge_index, 'kernel': _glorot(k0, D_IN, D_OUT), 'kernel1': _glorot(k1, D_IN, D_IN), 'kernel2': _glorot(k2, D_IN, D_IN), 'gamma': jnp.ones((D_IN,), jnp.float32), 'beta': jnp.zeros((D_IN,), jnp.float32)}
    _L3_gnn_all = _L3_gnn_setup()
    _L3_gnn_in = {k: v for k, v in _L3_gnn_all.items() if k in ('kernel', 'kernel1', 'kernel2', 'gamma', 'beta')}
    del _L3_gnn_all
    return {'x': x, 'src': src, 'dst': dst, 'edge_attr_128': edge_attr_128, 'edge_weight': edge_weight, 'L0_gnn_W1': _L0_gnn_in['W1'], 'L0_gnn_b1': _L0_gnn_in['b1'], 'L0_gnn_W2': _L0_gnn_in['W2'], 'L0_gnn_b2': _L0_gnn_in['b2'], 'L0_gnn_U1': _L0_gnn_in['U1'], 'L0_gnn_ub1': _L0_gnn_in['ub1'], 'L0_gnn_U2': _L0_gnn_in['U2'], 'L0_gnn_ub2': _L0_gnn_in['ub2'], 'L0_gnn_ln_w': _L0_gnn_in['ln_w'], 'L0_gnn_ln_b': _L0_gnn_in['ln_b'], 'L1_gnn_W1_l': _L1_gnn_in['W1_l'], 'L1_gnn_b1': _L1_gnn_in['b1'], 'L1_gnn_W1_r': _L1_gnn_in['W1_r'], 'L1_gnn_W2_l': _L1_gnn_in['W2_l'], 'L1_gnn_b2': _L1_gnn_in['b2'], 'L1_gnn_W2_r': _L1_gnn_in['W2_r'], 'L2_gnn_W1': _L2_gnn_in['W1'], 'L2_gnn_b1': _L2_gnn_in['b1'], 'L2_gnn_W2': _L2_gnn_in['W2'], 'L2_gnn_b2': _L2_gnn_in['b2'], 'L3_gnn_kernel': _L3_gnn_in['kernel'], 'L3_gnn_kernel1': _L3_gnn_in['kernel1'], 'L3_gnn_kernel2': _L3_gnn_in['kernel2'], 'L3_gnn_gamma': _L3_gnn_in['gamma'], 'L3_gnn_beta': _L3_gnn_in['beta']}

def reference(x, src, dst, edge_attr_128, edge_weight, L0_gnn_W1, L0_gnn_b1, L0_gnn_W2, L0_gnn_b2, L0_gnn_U1, L0_gnn_ub1, L0_gnn_U2, L0_gnn_ub2, L0_gnn_ln_w, L0_gnn_ln_b, L1_gnn_W1_l, L1_gnn_b1, L1_gnn_W1_r, L1_gnn_W2_l, L1_gnn_b2, L1_gnn_W2_r, L2_gnn_W1, L2_gnn_b1, L2_gnn_W2, L2_gnn_b2, L3_gnn_kernel, L3_gnn_kernel1, L3_gnn_kernel2, L3_gnn_gamma, L3_gnn_beta):
    import jax
    import jax.numpy as jnp

    def _L0_gnn_ref(node_features, edge_index, edge_features, W1, b1, W2, b2, U1, ub1, U2, ub2, ln_w, ln_b):
        import jax, jax.numpy as jnp
        import numpy as np
        N_NODES = 50000
        N_EDGES = 12500
        F_NODE = 128
        F_EDGE = 128
        HIDDEN = 128
        EPS = 1e-05

        def _glorot(key, shape):
            fan_in, fan_out = (shape[0], shape[1])
            lim = float(np.sqrt(6.0 / (fan_in + fan_out)))
            return jax.random.uniform(key, shape, jnp.float32, -lim, lim)
        src, dst = (edge_index[0], edge_index[1])
        message_input = jnp.concatenate([node_features[src], node_features[dst], edge_features], axis=-1)
        h = jax.nn.relu(message_input @ W1 + b1)
        messages = h @ W2 + b2
        aggregated = jax.ops.segment_sum(messages, dst, num_segments=node_features.shape[0])
        update_input = jnp.concatenate([node_features, aggregated], axis=-1)
        delta = jax.nn.relu(update_input @ U1 + ub1) @ U2 + ub2
        x = node_features + delta
        mu = jnp.mean(x, axis=-1, keepdims=True)
        var = jnp.var(x, axis=-1, keepdims=True)
        return (x - mu) * jax.lax.rsqrt(var + EPS) * ln_w + ln_b

    def _L1_gnn_ref(x, edge_index, W1_l, b1, W1_r, W2_l, b2, W2_r):
        import jax, jax.numpy as jnp
        import numpy as np

        def _sage_conv(h, src, dst, num_nodes, W_l, b, W_r):
            msg = h[src]
            agg = jax.ops.segment_sum(msg, dst, num_segments=num_nodes)
            deg = jax.ops.segment_sum(jnp.ones((src.shape[0],), h.dtype), dst, num_segments=num_nodes)
            agg = agg / jnp.maximum(deg, 1.0)[:, None]
            return agg @ W_l + b + h @ W_r
        src, dst = (edge_index[0], edge_index[1])
        N = x.shape[0]
        h = jax.nn.relu(_sage_conv(x, src, dst, N, W1_l, b1, W1_r))
        return _sage_conv(h, src, dst, N, W2_l, b2, W2_r)

    def _L2_gnn_ref(x, edge_index, edge_weight, W1, b1, W2, b2):
        import jax, jax.numpy as jnp
        import numpy as np
        N = 50000
        E = 12500
        D = 128

        def _gcn_layer(x, row, col, ew, W, b, n):
            deg = jax.ops.segment_sum(ew, col, num_segments=n)
            dis = jnp.where(deg > 0, jax.lax.rsqrt(jnp.maximum(deg, 1e-12)), 0.0)
            norm = dis[row] * ew * dis[col]
            h = x @ W
            msg = h[row] * norm[:, None]
            out = jax.ops.segment_sum(msg, col, num_segments=n)
            return out + b
        n = x.shape[0]
        loop = jnp.arange(n, dtype=edge_index.dtype)
        row = jnp.concatenate([edge_index[0], loop])
        col = jnp.concatenate([edge_index[1], loop])
        ew = jnp.concatenate([edge_weight, jnp.ones((n,), dtype=edge_weight.dtype)])
        h = _gcn_layer(x, row, col, ew, W1, b1, n)
        h = jax.nn.relu(h)
        out = _gcn_layer(h, row, col, ew, W2, b2, n)
        return out

    def _L3_gnn_ref(x, edge_index, kernel, kernel1, kernel2, gamma, beta):
        import jax, jax.numpy as jnp
        import numpy as np
        N_NODES = 100000
        D_IN = 128
        D_OUT = 128
        N_EDGES = 25000
        BN_EPS = 1e-05

        def _glorot(key, fan_in, fan_out):
            limit = np.sqrt(6.0 / (fan_in + fan_out))
            return jax.random.uniform(key, (fan_in, fan_out), jnp.float32, -limit, limit)
        N = x.shape[0]
        mean = jnp.mean(x, axis=0)
        var = jnp.var(x, axis=0)
        xn = (x - mean) * jax.lax.rsqrt(var + BN_EPS) * gamma + beta
        mapped = xn @ kernel
        s1 = jnp.tanh(jnp.sum(xn @ kernel1 * xn, axis=1))
        s2 = jnp.tanh(jnp.sum(xn @ kernel2 * xn, axis=1))
        src, dst = (edge_index[0], edge_index[1])
        e = jax.nn.leaky_relu(s1[src] + s2[dst], negative_slope=0.01)
        emax = jax.ops.segment_max(e, src, num_segments=N)
        emax = jnp.where(jnp.isfinite(emax), emax, 0.0)
        ee = jnp.exp(e - emax[src])
        denom = jax.ops.segment_sum(ee, src, num_segments=N)
        attn = ee / jnp.maximum(denom[src], 1e-16)
        out = jax.ops.segment_sum(attn[:, None] * mapped[dst], src, num_segments=N)
        return jax.nn.relu(out)
    edge_index = jnp.stack([src, dst])
    x = _layernorm(x + _L0_gnn_ref(x, edge_index, edge_attr_128, L0_gnn_W1, L0_gnn_b1, L0_gnn_W2, L0_gnn_b2, L0_gnn_U1, L0_gnn_ub1, L0_gnn_U2, L0_gnn_ub2, L0_gnn_ln_w, L0_gnn_ln_b), axis=-1)
    x = _layernorm(x + _L1_gnn_ref(x, edge_index, L1_gnn_W1_l, L1_gnn_b1, L1_gnn_W1_r, L1_gnn_W2_l, L1_gnn_b2, L1_gnn_W2_r), axis=-1)
    x = _layernorm(x + _L2_gnn_ref(x, edge_index, edge_weight, L2_gnn_W1, L2_gnn_b1, L2_gnn_W2, L2_gnn_b2), axis=-1)
    x = _layernorm(x + _L3_gnn_ref(x, edge_index, L3_gnn_kernel, L3_gnn_kernel1, L3_gnn_kernel2, L3_gnn_gamma, L3_gnn_beta), axis=-1)
    return x

_drawn_inputs = setup_inputs


def setup_inputs(seed=0):
    import zlib

    import numpy as np

    out = dict(_drawn_inputs(seed))
    spreads = {'L0_gnn_b1': (0.0, 0.8),
     'L0_gnn_b2': (0.0, 0.765),
     'L0_gnn_ub1': (0.0, 0.1),
     'L0_gnn_ub2': (0.0, 0.1),
     'L0_gnn_ln_w': (1.0, 0.2),
     'L0_gnn_ln_b': (0.0, 0.1),
     'L1_gnn_b1': (0.0, 0.1),
     'L1_gnn_b2': (0.0, 0.1),
     'L2_gnn_b1': (0.0, 0.1),
     'L2_gnn_b2': (0.0, 0.1),
     'L3_gnn_gamma': (1.0, 0.2),
     'L3_gnn_beta': (0.0, 0.304)}
    factors = {'L3_gnn_kernel1': 4.464, 'L3_gnn_kernel2': 3.138}
    for name, (base, spread) in spreads.items():
        noise = np.random.default_rng([zlib.crc32(name.encode()), seed]).standard_normal(out[name].shape)
        drawn = base * np.exp(spread * noise) if base else spread * noise
        out[name] = jnp.asarray(drawn.astype(out[name].dtype))
    for name, factor in factors.items():
        out[name] = (out[name] * factor).astype(out[name].dtype)
    return out
```

```python
from contextlib import ExitStack

import concourse.bass as bass
from concourse import mybir

ALU = mybir.AluOpType
ACT = mybir.ActivationFunctionType
AX = mybir.AxisListType
F32 = mybir.dt.float32
I32 = mybir.dt.int32
BF16 = mybir.dt.bfloat16

P = 128
D = 128
J = 4
GR = P * J
SLOTS = 7
EPS = 1e-5


class Steps:

    def __init__(self, sems, names, unit=1):
        self.sems, self.names, self.unit = sems, names, unit
        self.base = sems.base

    def after(self, name, i):
        return self.base + (self.names.index(name) + 1) * self.unit + i * (len(self.names) * self.unit)

    def all(self, i):
        return self.after(self.names[-1], i)

    def close(self, iters):
        self.sems.base += iters * len(self.names) * self.unit


class SlotSems(list):

    base = 0


def cols(t, j):
    return t.rearrange("f (p j) -> f j p", j=J)[:, j, :]


def rows(t, j):
    return t[:, j * D:(j + 1) * D]


def dram_rows(t, r, n=GR):
    return t[bass.ds(r, n), :].rearrange("(p j) f -> p (j f)", j=J)


def dram_vec(t, r, n=GR):
    return t[bass.ds(r, n)].rearrange("(p j) -> p j", j=J)


class K:
    pass


def build(nc, x, src, dst, edge_attr, edge_weight, w, out):
    N = x.shape[0]
    E = src.shape[0]
    EG = -(-E // (GR * SLOTS)) * SLOTS
    EP = EG * GR
    DG = -(-N // GR)
    assert EG == 49 and DG % SLOTS == 0 and x.shape[1] == D
    LO = 512
    PADNODE = -(-N // LO) * LO - 1
    DUMP = PADNODE + 1
    SLOTOF = DUMP + EP
    OOB = 1 << 20
    LO_CHUNKS = LO // P
    HI_CHUNKS = -(-((PADNODE // LO) + 1) // P)

    ctx = ExitStack()
    with ctx:
        k = K()

        def sb(name, shape, dt=F32):
            return ctx.enter_context(nc.sbuf_tensor(name, shape, dt))

        def sem(name):
            return ctx.enter_context(nc.semaphore(name))

        def slot_sems(name):
            return SlotSems(sem(f"{name}{b}") for b in range(SLOTS))

        def dram(name, shape, dt=F32):
            return nc.dram_tensor(name, shape, dt).ap()

        table = [dram(f"table{n}", [2 * EP, D]) for n in range(5)]
        X1, H1, X2S, H2S, X3 = range(5)
        x2_plain = dram("x2_plain", [EP, D])
        slot_of = dram("slot_of", [SLOTOF, 1], I32)
        dst_pad = dram("dst_pad", [EP + 2], I32)
        src_pad = dram("src_pad", [EP], I32)
        ew_pad = dram("ew_pad", [EP])
        edge_rows = dram("edge_rows", [EG, 4, GR])
        INV, MASK, EW, DIS = range(4)
        is_end = dram("is_end", [EP])
        dst_slot_idx = dram("dst_slot_idx", [EP], I32)
        edge_id = dram("edge_id", [EP], I32)
        src_gather_idx = dram("src_gather_idx", [EP], I32)
        dst_gather_idx = dram("dst_gather_idx", [EP], I32)
        src_found = dram("src_found", [EP], I32)
        src_row = dram("src_row", [EP], I32)
        dst_out_idx = dram("dst_out_idx", [EP], I32)
        digit = [dram(f"digit{n}", [EP]) for n in range(2)]
        record = [dram(f"record{n}", [EP, 4], I32) for n in range(3)]
        sorted_src = dram("sorted_src", [EP + 2], I32)
        sorted_mask = dram("sorted_mask", [EP])
        sorted_src_row = dram("sorted_src_row", [EP], I32)
        sorted_dst_row = dram("sorted_dst_row", [EP], I32)
        src_out_idx = dram("src_out_idx", [EP], I32)

        pe_done = slot_sems("pe_done")
        act_done = slot_sems("act_done")
        dve_done = slot_sems("dve_done")
        pool_done = slot_sems("pool_done")
        loaded = slot_sems("loaded")
        idx_loaded = slot_sems("idx_loaded")
        gathered = slot_sems("gathered")
        scattered = slot_sems("scattered")
        stored = slot_sems("stored")
        const_ready = sem("const_ready")
        weights_in = sem("weights_in")
        bias_split = sem("bias_split")
        dve_link = sem("dve_link")
        fill_ready = sem("fill_ready")
        pads_written = sem("pads_written")
        block_in = sem("block_in")
        iota_ready = sem("iota_ready")
        tails_ready = sem("tails_ready")
        tails_row = sem("tails_row")
        carry_row = sem("carry_row")
        carry_col = sem("carry_col")
        act_line = sem("act_line")
        sqrt_in = sem("sqrt_in")
        vectors_ready = sem("vectors_ready")
        vectors_written = sem("vectors_written")
        totals_ready = sem("totals_ready")
        bases_ready = sem("bases_ready")
        weights_total = 16 * (len(w["matrices"]) + len(w["columns"]) + 2 * J + len(w["rows"]))
        count = {}

        ident = sb("ident", [P, P])
        ones = sb("ones", [P, P])
        before = sb("before", [P, P])
        iota_bin = sb("iota_bin", [P, LO_CHUNKS])
        earlier = sb("earlier", [P, J, GR], BF16)
        eps = sb("eps", [P, 1])
        last_group_keep = sb("last_group_keep", [P, 1])
        W = {n: sb(f"w_{n}", [P, D]) for n in (
            "msg_src", "msg_dst", "msg_edge", "msg_out", "upd_x", "upd_agg", "upd_out",
            "sage1_l", "sage1_r", "sage2_l", "sage2_r", "gcn1", "gcn2", "map", "k1", "k2")}
        colb = {n: sb(f"c_{n}", [P, 1]) for n in ("msg_b1", "msg_b2", "upd_b1", "sage_b1", "gcn_b1", "gamma", "beta")}
        ln_w = sb("ln_w", [P, GR])
        ln_b = sb("ln_b", [P, GR])
        bias_rows = {n: sb(f"r_{n}", [3, GR], BF16) for n in ("upd_b2", "sage_b2", "gcn_b2")}
        ones_bf = sb("ones_bf", [3, P], BF16)
        bn_sum = sb("bn_sum", [P, 2])
        bn_a = sb("bn_a", [P, 1])
        bn_c = sb("bn_c", [P, 1])
        psum = [ctx.enter_context(nc.psum_tensor(f"bank{b}", [P, GR], F32)) for b in range(SLOTS)]
        spare = ctx.enter_context(nc.psum_tensor("bank_spare", [P, GR], F32))


        def reach(s, by=1):
            count[s] = count.get(s, 0) + by
            return count[s]

        def link(dve, ins):
            ins.then_inc(dve_link, 1)
            dve.wait_ge(dve_link, reach(dve_link))

        lo_pad = EP - E
        with (
            nc.sbuf_tensor("fill", [1, 2 * P], I32) as fill,
            nc.sbuf_tensor("fill_weight", [1, P], F32) as fill_weight,
            nc.sbuf_tensor("nothing", [P, SLOTOF // P], I32) as nothing,
            nc.sbuf_tensor("bias_in", [3, 3, D], F32) as bias_in,
            nc.sbuf_tensor("bias_tmp", [3, 4, D], F32) as bias_tmp,
            nc.sbuf_tensor("bias_hi", [3, D], BF16) as bias_hi,
            nc.Block() as block,
        ):
            assert SLOTOF % P == 0

            @block.gpsimd
            def _(pool):
                nc.gpsimd.memset(ident[:], 0.0).then_inc(const_ready, 1)
                nc.gpsimd.memset(ones[:], 1.0).then_inc(const_ready, 1)
                nc.gpsimd.memset(earlier[:], 1.0).then_inc(const_ready, 1)
                nc.gpsimd.memset(last_group_keep[:], 1.0).then_inc(const_ready, 1)
                pool.wait_ge(const_ready, 4)
                pool.affine_select(out=ident[:], in_=ident[:], compare_op=ALU.not_equal, fill=1.0, base=0,
                                   pattern=[[-1, P]], channel_multiplier=1).then_inc(const_ready, 1)
                pool.affine_select(out=before[:], in_=ones[:], compare_op=ALU.is_gt, fill=0.0, base=0,
                                   pattern=[[1, P]], channel_multiplier=-1).then_inc(const_ready, 1)
                pool.affine_select(out=earlier[:], in_=earlier[:], compare_op=ALU.is_gt, fill=0.0, base=0,
                                   pattern=[[1, J], [-1, GR]], channel_multiplier=J).then_inc(const_ready, 1)
                pool.affine_select(out=last_group_keep[:], in_=last_group_keep[:], compare_op=ALU.is_ge, fill=0.0,
                                   base=-((DG * GR - N) // J), pattern=[[0, 1]],
                                   channel_multiplier=1).then_inc(const_ready, 1)
                pool.iota(iota_bin[:], pattern=[[P, LO_CHUNKS]], base=0, channel_multiplier=1,
                          allow_small_or_imprecise_dtypes=True).then_inc(const_ready, 1)

            @block.vector
            def _(dve):
                nc.vector.memset(fill[0:1, 0:P], -1)
                nc.vector.memset(fill[0:1, P:2 * P], PADNODE)
                nc.vector.memset(fill_weight[:], 0.0)
                nc.vector.memset(nothing[:], -1).then_inc(fill_ready, 1)
                nc.vector.memset(ones_bf[:], 1.0)
                nc.vector.memset(eps[:], EPS)
                nc.vector.memset(bn_sum[:], 0.0)
                dve.wait_ge(const_ready, 9)
                dve.wait_ge(weights_in, weights_total)
                for n, name in enumerate(bias_rows):
                    whole = bias_in[:, n, :]
                    for part in range(3):
                        rest = whole if part == 0 else bias_tmp[:, part - 1, :]
                        link(dve, nc.vector.tensor_copy(bias_hi[:], rest))
                        if part < 2:
                            nc.vector.tensor_tensor(bias_tmp[:, part, :], rest, bias_hi[:], ALU.subtract)
                        mine = ident[0:3, part:part + 1]
                        if part == 0:
                            link(dve, nc.vector.tensor_scalar(bias_tmp[:, 3, :], bias_hi[:], mine, None, ALU.mult))
                        else:
                            link(dve, nc.vector.scalar_tensor_tensor(out=bias_tmp[:, 3, :], in0=bias_hi[:], scalar=mine,
                                                                     in1=bias_tmp[:, 3, :], op0=ALU.mult, op1=ALU.add))
                    for j in range(J):
                        link(dve, nc.vector.tensor_copy(bias_rows[name][:, j * D:(j + 1) * D], bias_tmp[:, 3, :]))

            @block.sync
            def _(sp):
                for name, source in w["matrices"].items():
                    sp.dma_start(W[name][:], source).then_inc(weights_in, 16)
                for name, source in w["columns"].items():
                    sp.dma_start(colb[name][:], source.rearrange("(p a) -> p a", a=1)).then_inc(weights_in, 16)
                for j in range(J):
                    sp.dma_start(ln_w[:, j * D:(j + 1) * D], w["ln_w"].partition_broadcast(P)).then_inc(weights_in, 16)
                    sp.dma_start(ln_b[:, j * D:(j + 1) * D], w["ln_b"].partition_broadcast(P)).then_inc(weights_in, 16)
                for n, name in enumerate(bias_rows):
                    sp.dma_start(bias_in[:, n, :], w["rows"][name].partition_broadcast(3)).then_inc(weights_in, 16)
                sp.dma_start(dst_pad[1:1 + E], dst).then_inc(pads_written, 16)
                sp.dma_start(src_pad[0:E], src).then_inc(pads_written, 16)
                sp.dma_start(ew_pad[0:E], edge_weight).then_inc(pads_written, 16)
                sp.wait_ge(fill_ready, 1)
                def as_row(v, first, n):
                    return v[first:first + n].rearrange("(a n) -> a n", a=1)

                minus_one = fill[0:1, 0:1]
                sp.dma_start(as_row(dst_pad, 0, 1), minus_one).then_inc(pads_written, 16)
                sp.dma_start(as_row(dst_pad, 1 + E, lo_pad), fill[0:1, P:P + lo_pad]).then_inc(pads_written, 16)
                sp.dma_start(as_row(dst_pad, 1 + EP, 1), minus_one).then_inc(pads_written, 16)
                sp.dma_start(as_row(sorted_src, 0, 1), minus_one).then_inc(pads_written, 16)
                sp.dma_start(as_row(sorted_src, 1 + EP, 1), minus_one).then_inc(pads_written, 16)
                sp.dma_start(as_row(src_pad, E, lo_pad), fill[0:1, P:P + lo_pad]).then_inc(pads_written, 16)
                sp.dma_start(as_row(ew_pad, E, lo_pad), fill_weight[0:1, 0:lo_pad]).then_inc(pads_written, 16)
                sp.dma_start(slot_of.rearrange("(p n) a -> p (n a)", p=P), nothing[:]).then_inc(pads_written, 16)
                sp.wait_ge(pads_written, 11 * 16)
                sp.wait_ge(weights_in, weights_total)

        def block_view(v, first=0):
            return v[first:first + EP].rearrange("(g c) -> g c", g=EG)

        with ExitStack() as part:
            def tile(name, dt=F32, width=GR):
                return part.enter_context(nc.sbuf_tensor(name, [EG, width], dt))

            dst_i, prev_i, next_i, src_i = (tile(n, I32) for n in ("dst_i", "prev_i", "next_i", "src_i"))
            weight = tile("weight")
            edge_i = tile("edge_i", I32)
            edge_f, mask, go_on, end, zero, one_f = (tile(n) for n in ("edge_f", "mask", "go_on", "end", "zero", "one_f"))
            local = [tile(f"local{n}") for n in range(3)]
            runs = [tile(f"runs{n}") for n in range(2)]
            total = [tile(f"total{n}") for n in range(3)]
            tmp, tmp2 = tile("tmp"), tile("tmp2")
            int_total = tile("int_total", I32)
            int_out = [tile(f"int_out{n}", I32) for n in range(4)]
            tail_rows = part.enter_context(nc.sbuf_tensor("tail_rows", [1, 2, EG], F32))
            carry = part.enter_context(nc.sbuf_tensor("carry", [1, EG], F32))
            sums = part.enter_context(nc.sbuf_tensor("sums", [1, EG], F32))
            block = part.enter_context(nc.Block())

            scans = [(0, 0, GR - 1), (1, 0, GR - 1), (2, 1, 0)]

            @block.sync
            def _(sp):
                for t, v, first in ((dst_i, dst_pad, 1), (prev_i, dst_pad, 0), (next_i, dst_pad, 2),
                                    (src_i, src_pad, 0), (weight, ew_pad, 0)):
                    sp.dma_start(t[:], block_view(v, first)).then_inc(block_in, 16)
                sp.wait_ge(vectors_ready, 1)
                for r, t in ((INV, total[0]), (MASK, mask), (EW, weight), (DIS, total[1])):
                    sp.dma_start(edge_rows[:, r, :], t[:]).then_inc(vectors_written, 16)
                sp.dma_start(block_view(is_end), end[:]).then_inc(vectors_written, 16)
                sp.dma_start(block_view(edge_id), edge_i[:]).then_inc(vectors_written, 16)
                for v, t in zip((dst_slot_idx, dst_gather_idx, src_gather_idx, dst_out_idx), int_out):
                    sp.dma_start(block_view(v), t[:]).then_inc(vectors_written, 16)
                sp.dma_start(block_view(sorted_dst_row), int_total[:]).then_inc(vectors_written, 16)
                sp.wait_ge(vectors_written, 11 * 16)

            @block.gpsimd
            def _(pool):
                pool.iota(edge_i[:], pattern=[[1, GR]], base=0, channel_multiplier=GR).then_inc(iota_ready, 1)

            @block.tensor
            def _(pe):
                for n, (v, m, last) in enumerate(scans):
                    pe.wait_ge(tails_ready, n + 1)
                    nc.tensor.matmul(spare[0:1, 0:EG], local[v][:, last:last + 1], ident[0:EG, 0:EG], start=True, stop=True)
                    nc.tensor.matmul(spare[0:1, P:P + EG], runs[m][:, last:last + 1], ident[0:EG, 0:EG],
                                     start=True, stop=True).then_inc(tails_row, 1)
                    pe.wait_ge(carry_row, n + 1)
                    nc.tensor.matmul(spare[0:EG, 2 * P:2 * P + 1], carry[0:1, :], ones[0:1, 0:1],
                                     start=True, stop=True).then_inc(carry_col, 1)

            @block.scalar
            def _(act):
                act.wait_ge(sqrt_in, 1)
                nc.scalar.activation(tmp2[:], tmp[:], ACT.Sqrt).then_inc(act_line, 1)

            @block.vector
            def _(dve):
                nc.vector.memset(zero[:], 0.0)
                link(dve, nc.vector.memset(one_f[:], 1.0))
                dve.wait_ge(block_in, 5 * 16)
                dve.wait_ge(iota_ready, 1)
                nc.vector.tensor_copy(edge_f[:], edge_i[:])
                nc.vector.tensor_tensor(mask[:], dst_i[:], prev_i[:], ALU.is_equal)
                nc.vector.tensor_tensor(go_on[:], dst_i[:], next_i[:], ALU.is_equal)
                link(dve, nc.vector.tensor_tensor(end[:], dst_i[:], next_i[:], ALU.not_equal))
                link(dve, nc.vector.tensor_tensor(tmp[:], edge_f[:], end[:], ALU.mult))
                nc.vector.tensor_tensor_scan(local[0][:], mask[:], one_f[:], 0.0, ALU.mult, ALU.add)
                nc.vector.tensor_tensor_scan(local[1][:], mask[:], weight[:], 0.0, ALU.mult, ALU.add)
                nc.vector.tensor_tensor_scan(local[2][:, ::-1], go_on[:, ::-1], tmp[:, ::-1], 0.0, ALU.mult, ALU.add)
                nc.vector.tensor_tensor_scan(runs[0][:], mask[:], zero[:], 1.0, ALU.mult, ALU.add)
                link(dve, nc.vector.tensor_tensor_scan(runs[1][:, ::-1], go_on[:, ::-1], zero[:, ::-1], 1.0, ALU.mult, ALU.add))
                for n, (v, m, last) in enumerate(scans):
                    nc.vector.memset(carry[:], 0.0).then_inc(tails_ready, 1)
                    dve.wait_ge(tails_row, n + 1)
                    nc.vector.tensor_copy(tail_rows[0:1, 0, :], spare[0:1, 0:EG])
                    link(dve, nc.vector.tensor_copy(tail_rows[0:1, 1, :], spare[0:1, P:P + EG]))
                    if last:
                        link(dve, nc.vector.tensor_tensor_scan(sums[:], tail_rows[0:1, 1, :], tail_rows[0:1, 0, :], 0.0,
                                                               ALU.mult, ALU.add))
                        nc.vector.tensor_copy(carry[0:1, 1:EG], sums[0:1, 0:EG - 1]).then_inc(carry_row, 1)
                    else:
                        link(dve, nc.vector.tensor_tensor_scan(sums[0:1, ::-1], tail_rows[0:1, 1, ::-1],
                                                               tail_rows[0:1, 0, ::-1], 0.0, ALU.mult, ALU.add))
                        nc.vector.tensor_copy(carry[0:1, 0:EG - 1], sums[0:1, 1:EG]).then_inc(carry_row, 1)
                    dve.wait_ge(carry_col, n + 1)
                    link(dve, nc.vector.scalar_tensor_tensor(out=total[v][:], in0=runs[m][:],
                                                             scalar=spare[0:EG, 2 * P:2 * P + 1],
                                                             in1=local[v][:], op0=ALU.mult, op1=ALU.add))
                nc.vector.tensor_copy(int_total[:], total[2][:])
                link(dve, nc.vector.tensor_scalar(total[0][:], total[0][:], 1.0, None, ALU.max))
                link(dve, nc.vector.reciprocal(total[0][:], total[0][:]))
                link(dve, nc.vector.tensor_scalar(total[1][:], total[1][:], 1.0, None, ALU.add))
                nc.vector.tensor_scalar(tmp[:], total[1][:], 1e-12, None, ALU.max).then_inc(sqrt_in, 1)
                dve.wait_ge(act_line, 1)
                link(dve, nc.vector.reciprocal(tmp2[:], tmp2[:]))
                link(dve, nc.vector.scalar_tensor_tensor(out=total[1][:], in0=total[1][:], scalar=0.0, in1=tmp2[:],
                                                         op0=ALU.is_gt, op1=ALU.mult))
                link(dve, nc.vector.tensor_scalar(tmp[:], edge_f[:], float(DUMP), None, ALU.add))
                link(dve, nc.vector.tensor_tensor(tmp2[:], dst_i[:], tmp[:], ALU.subtract))
                link(dve, nc.vector.tensor_tensor(tmp2[:], tmp2[:], end[:], ALU.mult))
                nc.vector.tensor_tensor(int_out[0][:], tmp2[:], tmp[:], ALU.add)
                nc.vector.tensor_scalar(int_out[1][:], dst_i[:], float(N - 1), None, ALU.min)
                link(dve, nc.vector.tensor_scalar(int_out[2][:], src_i[:], float(N - 1), None, ALU.min))
                link(dve, nc.vector.tensor_scalar(tmp2[:], dst_i[:], float(N), None, ALU.is_lt))
                link(dve, nc.vector.tensor_tensor(tmp2[:], tmp2[:], end[:], ALU.mult))
                link(dve, nc.vector.tensor_scalar(tmp[:], dst_i[:], float(-OOB), None, ALU.add))
                link(dve, nc.vector.tensor_tensor(tmp[:], tmp[:], tmp2[:], ALU.mult))
                nc.vector.tensor_scalar(int_out[3][:], tmp[:], float(OOB), None, ALU.add).then_inc(vectors_ready, 1)

        S = range(SLOTS)
        EDGE_ITERS = EG // SLOTS
        DENSE_ITERS = DG // SLOTS

        def at(i, b):
            return i * (SLOTS * GR) + b * GR

        def wait_alone(eng, s, value):
            eng.wait_ge(s, value)
            eng.nop(nofuse=True)

        def gather(pool, rows_out, idx, source, j, s):
            pool.indirect_dma_start(out=rows_out, out_offset=None, in_=source,
                                    in_offset=bass.IndirectOffsetOnAxis(ap=idx[:, j:j + 1], axis=0)).then_inc(s, 16)

        def scatter(pool, target, idx, rows_in, j, s, limit=None):
            more = {} if limit is None else {"bounds_check": limit, "oob_is_err": False}
            pool.indirect_dma_start(out=target, out_offset=bass.IndirectOffsetOnAxis(ap=idx[:, j:j + 1], axis=0),
                                    in_=rows_in, in_offset=None, **more).then_inc(s, 16)

        with ExitStack() as part:
            idx = [part.enter_context(nc.sbuf_tensor(f"end_idx{b}", [P, J], I32)) for b in S]
            val = [part.enter_context(nc.sbuf_tensor(f"end_val{b}", [P, J], I32)) for b in S]
            LD = Steps(idx_loaded, ["idx", "val"], 16)
            SC = Steps(scattered, [f"scatter{j}" for j in range(J)], 16)
            block = part.enter_context(nc.Block())

            @block.sync
            def _(sp):
                def load(i, b):
                    sp.dma_start(idx[b][:], dram_vec(dst_slot_idx, at(i, b))).then_inc(idx_loaded[b], 16)
                    sp.dma_start(val[b][:], dram_vec(edge_id, at(i, b))).then_inc(idx_loaded[b], 16)

                for b in S:
                    load(0, b)
                with sp.Fori(0, EDGE_ITERS - 1) as i:
                    for b in S:
                        sp.wait_ge(scattered[b], SC.all(i))
                        load(i + 1, b)
                for b in S:
                    sp.wait_ge(scattered[b], SC.all(EDGE_ITERS - 1))

            @block.gpsimd
            def _(pool):
                with pool.Fori(0, EDGE_ITERS) as i:
                    for b in S:
                        wait_alone(pool, idx_loaded[b], LD.all(i))
                        for j in range(J):
                            scatter(pool, slot_of, idx[b], val[b][:, j:j + 1], j, scattered[b])

            LD.close(EDGE_ITERS)
            SC.close(EDGE_ITERS)

        with ExitStack() as part:
            idx = [part.enter_context(nc.sbuf_tensor(f"src_idx{b}", [P, J], I32)) for b in S]
            val = [part.enter_context(nc.sbuf_tensor(f"src_val{b}", [P, J], I32)) for b in S]
            LD = Steps(idx_loaded, ["idx"], 16)
            GA = Steps(gathered, [f"gather{j}" for j in range(J)], 16)
            ST = Steps(stored, ["found"], 16)
            block = part.enter_context(nc.Block())

            @block.sync
            def _(sp):
                def load(i, b):
                    sp.dma_start(idx[b][:], dram_vec(src_pad, at(i, b))).then_inc(idx_loaded[b], 16)

                def store(i, b):
                    sp.wait_ge(gathered[b], GA.all(i))
                    sp.dma_start(dram_vec(src_found, at(i, b)), val[b][:]).then_inc(stored[b], 16)

                for b in S:
                    load(0, b)
                with sp.Fori(0, EDGE_ITERS - 1) as i:
                    for b in S:
                        store(i, b)
                    for b in S:
                        sp.wait_ge(stored[b], ST.all(i))
                        load(i + 1, b)
                for b in S:
                    store(EDGE_ITERS - 1, b)
                for b in S:
                    sp.wait_ge(stored[b], ST.all(EDGE_ITERS - 1))

            @block.gpsimd
            def _(pool):
                with pool.Fori(0, EDGE_ITERS) as i:
                    for b in S:
                        wait_alone(pool, idx_loaded[b], LD.all(i))
                        for j in range(J):
                            gather(pool, val[b][:, j:j + 1], idx[b], slot_of, j, gathered[b])

            LD.close(EDGE_ITERS)
            GA.close(EDGE_ITERS)
            ST.close(EDGE_ITERS)

        with ExitStack() as part:
            def tile(name, dt=F32, width=GR):
                return part.enter_context(nc.sbuf_tensor(name, [EG, width], dt))

            found, src_i, end_i, edge_i, row_i = (tile(n, I32) for n in ("found", "src_i2", "end_i", "edge_i2", "row_i"))
            digit_i = [tile(f"digit_i{n}", I32) for n in range(2)]
            low_f = tile("low_f")
            own, has, pick = tile("own"), tile("has"), tile("pick")
            rec = tile("rec", I32, 4 * GR)
            field = rec[:].rearrange("g (c f) -> g f c", f=4)
            in2, out2 = sem("sources_in"), sem("sources_out")
            block = part.enter_context(nc.Block())

            @block.sync
            def _(sp):
                for t, v in ((found, src_found), (src_i, src_pad), (end_i, sorted_dst_row), (edge_i, edge_id)):
                    sp.dma_start(t[:], block_view(v)).then_inc(in2, 16)
                sp.wait_ge(vectors_ready, 2)
                sp.dma_start(block_view(src_row), row_i[:]).then_inc(out2, 16)
                sp.dma_start(block_view(digit[0]), low_f[:]).then_inc(out2, 16)
                sp.dma_start(record[0].rearrange("(g c) f -> g (c f)", g=EG), rec[:]).then_inc(out2, 16)
                sp.wait_ge(out2, 48)

            @block.vector
            def _(dve):
                dve.wait_ge(in2, 64)
                nc.vector.tensor_scalar(has[:], found[:], 0.0, None, ALU.is_ge)
                nc.vector.tensor_scalar(digit_i[0][:], src_i[:], LO - 1, None, ALU.bitwise_and)
                nc.vector.tensor_scalar(digit_i[1][:], src_i[:], LO.bit_length() - 1, None, ALU.logical_shift_right)
                link(dve, nc.vector.tensor_scalar(own[:], edge_i[:], float(EP), None, ALU.add))
                link(dve, nc.vector.tensor_tensor(pick[:], found[:], own[:], ALU.subtract))
                link(dve, nc.vector.tensor_tensor(pick[:], pick[:], has[:], ALU.mult))
                link(dve, nc.vector.tensor_tensor(row_i[:], pick[:], own[:], ALU.add))
                nc.vector.tensor_copy(low_f[:], digit_i[0][:])
                nc.vector.tensor_copy(field[:, 0, :], digit_i[1][:])
                nc.vector.tensor_copy(field[:, 1, :], src_i[:])
                nc.vector.tensor_copy(field[:, 2, :], row_i[:])
                nc.vector.tensor_copy(field[:, 3, :], end_i[:]).then_inc(vectors_ready, 1)

        def sort_pass(n, chunks):
            with ExitStack() as part:
                def slots(name, shape, dt=F32):
                    return [part.enter_context(nc.sbuf_tensor(f"{name}{n}_{b}", shape, dt)) for b in S]

                dig = slots("dig", [P, GR])
                dig_col = slots("dig_col", [P, J])
                rec = slots("rec", [P, J * 4], I32)
                hot = slots("hot", [P, chunks, GR])
                same = slots("same", [P, J, GR], BF16)
                inner = slots("inner", [P, J])
                rank = slots("rank", [P, J], I32)
                hist = part.enter_context(nc.sbuf_tensor(f"hist{n}", [P, chunks, EG], F32))
                first = part.enter_context(nc.sbuf_tensor(f"first{n}", [P, chunks, EG], F32))
                sums = part.enter_context(nc.sbuf_tensor(f"bin_sums{n}", [P, chunks, EG], F32))
                ones_g = part.enter_context(nc.sbuf_tensor(f"ones_g{n}", [P, EG], F32))
                lower = part.enter_context(nc.sbuf_tensor(f"lower{n}", [P, chunks], F32))

                LD = Steps(loaded, ["digits"], 16)
                DV = Steps(dve_done, ["count"])
                with nc.Block() as block:
                    @block.sync
                    def _(sp):
                        def load(i, b):
                            sp.dma_start(dig[b][:], digit[n][bass.ds(at(i, b), GR)].partition_broadcast(P))\
                              .then_inc(loaded[b], 16)

                        for b in S:
                            load(0, b)
                        with sp.Fori(0, EDGE_ITERS - 1) as i:
                            for b in S:
                                sp.wait_ge(dve_done[b], DV.all(i))
                                load(i + 1, b)

                    @block.vector
                    def _(dve):
                        with dve.Fori(0, EDGE_ITERS) as i:
                            for b in S:
                                dve.wait_ge(loaded[b], LD.all(i))
                                for c in range(chunks):
                                    ins = nc.vector.tensor_scalar(
                                        hot[b][:, c, :], dig[b][:], iota_bin[:, c:c + 1], None, ALU.is_equal, ALU.add,
                                        accum_out=hist[:, c, bass.ds(i * SLOTS + b, 1)])
                                ins.then_inc(dve_done[b], 1)
                LD.close(EDGE_ITERS)
                DV.close(EDGE_ITERS)

                with nc.Block() as block:
                    @block.vector
                    def _(dve):
                        link(dve, nc.vector.memset(ones_g[:], 1.0))
                        for c in range(chunks):
                            link(dve, nc.vector.tensor_tensor_scan(sums[:, c, :], ones_g[:], hist[:, c, :], 0.0,
                                                                   ALU.mult, ALU.add))
                        link(dve, nc.vector.tensor_tensor(first[:], sums[:], hist[:], ALU.subtract))
                        link(dve, nc.vector.memset(lower[:], 0.0))
                        for c in range(1, chunks):
                            link(dve, nc.vector.tensor_tensor(lower[:, c:c + 1], lower[:, c - 1:c],
                                                              sums[:, c - 1, EG - 1:EG], ALU.add))
                        nc.vector.tensor_copy(inner[0][:, 0:chunks], sums[:, :, EG - 1]).then_inc(totals_ready, 1)
                        dve.wait_ge(bases_ready, n + 1)
                        for c in range(chunks):
                            link(dve, nc.vector.tensor_scalar(first[:, c, :], first[:, c, :], spare[:, c:c + 1], None, ALU.add))

                    @block.tensor
                    def _(pe):
                        pe.wait_ge(totals_ready, n + 1)
                        nc.tensor.matmul(spare[:, 0:chunks], before[:], inner[0][:, 0:chunks], start=True, stop=False)
                        nc.tensor.matmul(spare[:, 0:chunks], ones[:], lower[:], start=False, stop=True)\
                          .then_inc(bases_ready, 1)

                LD = Steps(loaded, ["digits", "columns", "records"], 16)
                DV = Steps(dve_done, ["hot", "inner", "rank"])
                PE = Steps(pe_done, ["lookup"])
                SC = Steps(scattered, [f"record{j}" for j in range(J)], 16)
                with nc.Block() as block:
                    @block.sync
                    def _(sp):
                        def load(i, b):
                            sp.dma_start(dig[b][:], digit[n][bass.ds(at(i, b), GR)].partition_broadcast(P))\
                              .then_inc(loaded[b], 16)
                            sp.dma_start(dig_col[b][:], dram_vec(digit[n], at(i, b))).then_inc(loaded[b], 16)
                            sp.dma_start(rec[b][:], record[n][bass.ds(at(i, b), GR), :]
                                         .rearrange("(p j) f -> p (j f)", j=J)).then_inc(loaded[b], 16)

                        for b in S:
                            load(0, b)
                        with sp.Fori(0, EDGE_ITERS - 1) as i:
                            for b in S:
                                sp.wait_ge(scattered[b], SC.all(i))
                                load(i + 1, b)
                        for b in S:
                            sp.wait_ge(scattered[b], SC.all(EDGE_ITERS - 1))

                    @block.vector
                    def _(dve):
                        with dve.Fori(0, EDGE_ITERS) as i:
                            for b in S:
                                dve.wait_ge(loaded[b], LD.all(i))
                                for c in range(chunks):
                                    ins = nc.vector.tensor_scalar(hot[b][:, c, :], dig[b][:], iota_bin[:, c:c + 1], None,
                                                                  ALU.is_equal)
                                ins.then_inc(dve_done[b], 1)
                            for b in S:
                                for j in range(J):
                                    ins = nc.vector.scalar_tensor_tensor(
                                        out=same[b][:, j, :], in0=dig[b][:], scalar=dig_col[b][:, j:j + 1],
                                        in1=earlier[:, j, :], op0=ALU.is_equal, op1=ALU.mult,
                                        accum_out=inner[b][:, j:j + 1])
                                ins.then_inc(dve_done[b], 1)
                            for b in S:
                                dve.wait_ge(pe_done[b], PE.after("lookup", i))
                                dve.wait_ge(dve_done[b], DV.after("inner", i))
                                nc.vector.tensor_tensor(rank[b][:], psum[b][:, 0:J], inner[b][:], ALU.add)\
                                  .then_inc(dve_done[b], 1)

                    @block.tensor
                    def _(pe):
                        with pe.Fori(0, EDGE_ITERS) as i:
                            for b in S:
                                pe.wait_ge(dve_done[b], DV.after("hot", i))
                                for j in range(J):
                                    for c in range(chunks):
                                        ins = nc.tensor.matmul(psum[b][:, j:j + 1], cols(hot[b][:, c, :], j),
                                                               first[:, c, bass.ds(i * SLOTS + b, 1)],
                                                               start=(c == 0), stop=(c == chunks - 1))
                                ins.then_inc(pe_done[b], 1)

                    @block.gpsimd
                    def _(pool):
                        with pool.Fori(0, EDGE_ITERS) as i:
                            for b in S:
                                wait_alone(pool, dve_done[b], DV.after("rank", i))
                                for j in range(J):
                                    scatter(pool, record[n + 1], rank[b], rec[b][:, 4 * j:4 * j + 4], j, scattered[b])
                LD.close(EDGE_ITERS)
                DV.close(EDGE_ITERS)
                PE.close(EDGE_ITERS)
                SC.close(EDGE_ITERS)

        sort_pass(0, LO_CHUNKS)

        with ExitStack() as part:
            rec = part.enter_context(nc.sbuf_tensor("rec1", [EG, 4 * GR], I32))
            high = part.enter_context(nc.sbuf_tensor("high", [EG, GR], F32))
            in3, out3, high_ready = sem("rec1_in"), sem("high_out"), sem("high_ready")
            block = part.enter_context(nc.Block())

            @block.sync
            def _(sp):
                sp.dma_start(rec[:], record[1].rearrange("(g c) f -> g (c f)", g=EG)).then_inc(in3, 16)
                sp.wait_ge(high_ready, 1)
                sp.dma_start(block_view(digit[1]), high[:]).then_inc(out3, 16)
                sp.wait_ge(out3, 16)

            @block.vector
            def _(dve):
                dve.wait_ge(in3, 16)
                nc.vector.tensor_copy(high[:], rec[:].rearrange("g (c f) -> g f c", f=4)[:, 0, :]).then_inc(high_ready, 1)

        sort_pass(1, HI_CHUNKS)

        with ExitStack() as part:
            def tile(name, dt=F32, width=GR):
                return part.enter_context(nc.sbuf_tensor(name, [EG, width], dt))

            rec = tile("rec2", I32, 4 * GR)
            src_s, prev_s, next_s, row_s, end_s, out_s = (tile(n, I32) for n in
                                                          ("src_s", "prev_s", "next_s", "row_s", "end_s", "out_s"))
            mask, end, tmp, tmp2 = (tile(n) for n in ("mask_s", "end_flag_s", "tmp_s", "tmp2_s"))
            in4, out4, fields, around, done4 = (sem(n) for n in ("rec2_in", "sorted_out", "fields", "around", "sorted_done"))
            field = rec[:].rearrange("g (c f) -> g f c", f=4)
            block = part.enter_context(nc.Block())

            @block.sync
            def _(sp):
                sp.dma_start(rec[:], record[2].rearrange("(g c) f -> g (c f)", g=EG)).then_inc(in4, 16)
                sp.wait_ge(fields, 1)
                sp.dma_start(block_view(sorted_src, 1), src_s[:]).then_inc(out4, 16)
                sp.dma_start(block_view(sorted_src_row), row_s[:]).then_inc(out4, 16)
                sp.dma_start(block_view(sorted_dst_row), end_s[:]).then_inc(out4, 16)
                sp.wait_ge(out4, 48)
                sp.dma_start(prev_s[:], block_view(sorted_src, 0)).then_inc(around, 16)
                sp.dma_start(next_s[:], block_view(sorted_src, 2)).then_inc(around, 16)
                sp.wait_ge(done4, 1)
                sp.dma_start(block_view(sorted_mask), mask[:]).then_inc(out4, 16)
                sp.dma_start(block_view(src_out_idx), out_s[:]).then_inc(out4, 16)
                sp.wait_ge(out4, 80)

            @block.vector
            def _(dve):
                dve.wait_ge(in4, 16)
                nc.vector.tensor_copy(src_s[:], field[:, 1, :])
                nc.vector.tensor_copy(row_s[:], field[:, 2, :])
                nc.vector.tensor_copy(end_s[:], field[:, 3, :]).then_inc(fields, 1)
                dve.wait_ge(around, 32)
                nc.vector.tensor_tensor(mask[:], src_s[:], prev_s[:], ALU.is_equal)
                nc.vector.tensor_tensor(end[:], src_s[:], next_s[:], ALU.not_equal)
                nc.vector.tensor_scalar(tmp[:], src_s[:], float(-OOB), None, ALU.add)
                link(dve, nc.vector.tensor_scalar(tmp2[:], src_s[:], float(N), None, ALU.is_lt))
                link(dve, nc.vector.tensor_tensor(tmp2[:], tmp2[:], end[:], ALU.mult))
                link(dve, nc.vector.tensor_tensor(tmp[:], tmp[:], tmp2[:], ALU.mult))
                nc.vector.tensor_scalar(out_s[:], tmp[:], float(OOB), None, ALU.add).then_inc(done4, 1)

        def tiles(part, name, *names, width=GR, dt=F32):
            return [[part.enter_context(nc.sbuf_tensor(f"{name}_{n}{b}", [P, width], dt)) for b in S] for n in names]

        def run_sync(sp, iters, load, store, free):
            for b in S:
                load(0, b)

            def body(i):
                store(i)
                for b in S:
                    free(i, b)
                    load(i + 1, b)

            with sp.Fori(0, iters - 2) as i:
                body(i)
            body(iters - 2)
            store(iters - 1)
            for b in S:
                free(iters - 1, b)

        def pe_to_cols(b, source):
            for j in range(J):
                ins = nc.tensor.transpose(cols(psum[b][:], j), rows(source, j), ident[:])
            return ins

        def pe_to_rows(b, source):
            for j in range(J):
                ins = nc.tensor.transpose(rows(psum[b], j), cols(source[:], j), ident[:])
            return ins

        def pe_features(b, *terms):
            for n, (name, xT) in enumerate(terms):
                weight = ones if name == "ones" else W[name]
                ins = nc.tensor.matmul(psum[b][:], weight[:], xT[:], start=(n == 0), stop=(n == len(terms) - 1))
            return ins

        def pe_nodes(b, bias, *terms):
            if bias:
                nc.tensor.matmul(psum[b][:], ones_bf[:], bias_rows[bias][:], start=True, stop=False)
            for j in range(J):
                for n, (name, xT) in enumerate(terms):
                    last = n == len(terms) - 1 and (not bias or j == J - 1)
                    ins = nc.tensor.matmul(rows(psum[b], j), cols(xT[:], j), W[name][:],
                                           start=(not bias and n == 0), stop=last)
            return ins

        def pe_sums(b, x3, squares, keep):
            for c, t in enumerate((x3, squares)):
                for j in range(J):
                    ins = nc.tensor.matmul(psum[b][:, c:c + 1], rows(t, j), keep[:, j:j + 1],
                                           start=(j == 0), stop=(j == J - 1))
            return ins

        moments = [sb(f"moments{b}", [P, J, 2]) for b in S]
        stats = [sb(f"stats{b}", [P, J, 6]) for b in S]
        root = [sb(f"root{b}", [P, J]) for b in S]
        bn_part = [sb(f"bn_part{b}", [P, 2]) for b in S]

        def norm_dve(name):
            return [f"{name}_stats", f"{name}_moments", f"{name}_inv", f"{name}_norm"]

        def dve_stats(dve, DV, name, i, source, before):
            for b in S:
                dve.wait_ge(dve_done[b], DV.after(before, i))
                for j in range(J):
                    ins = nc.vector.bn_stats(stats[b][:, j, :], rows(source[b], j))
                ins.then_inc(dve_done[b], 1)
            for b in S:
                wait_alone(dve, dve_done[b], DV.after(f"{name}_stats", i))
                for j in range(J):
                    ins = nc.vector.bn_aggr(moments[b][:, j, :], stats[b][:, j, :])
                ins.then_inc(dve_done[b], 1)

        def act_root(act, DV, name, i):
            for b in S:
                act.wait_ge(dve_done[b], DV.after(f"{name}_moments", i))
                nc.scalar.activation(root[b][:], moments[b][:, :, 1], ACT.Sqrt, bias=eps[:]).then_inc(act_done[b], 1)

        def dve_norm(dve, DV, AC, name, i, source, target):
            for b in S:
                dve.wait_ge(act_done[b], AC.after(f"{name}_root", i))
                nc.vector.reciprocal(root[b][:], root[b][:]).then_inc(dve_done[b], 1)
            for b in S:
                dve.wait_ge(dve_done[b], DV.after(f"{name}_inv", i))
                for j in range(J):
                    ins = nc.vector.tensor_scalar(rows(target[b], j), rows(source[b], j), moments[b][:, j, 0:1],
                                                  root[b][:, j:j + 1], ALU.subtract, ALU.mult)
                ins.then_inc(dve_done[b], 1)

        def act_copy(act, PE, name, i, target, func=ACT.Copy, **more):
            for b in S:
                act.wait_ge(pe_done[b], PE.after(name, i))
                nc.scalar.activation(target[b][:], psum[b][:], func, **more).then_inc(act_done[b], 1)

        def dve_affine(dve, DV, i, z, xb, pool_steps):
            for b in S:
                dve.wait_ge(dve_done[b], DV.after("ln0_norm", i))
                nc.vector.tensor_tensor(z[b][:], z[b][:], ln_w[:], ALU.mult).then_inc(dve_done[b], 1)
            for b in S:
                dve.wait_ge(dve_done[b], DV.after("ln0_w", i))
                dve.wait_ge(pool_done[b], pool_steps.after("xb", i))
                nc.vector.tensor_tensor(z[b][:], z[b][:], xb[b][:], ALU.add).then_inc(dve_done[b], 1)

        def dve_residual(dve, PE, name, i, z, x):
            for b in S:
                dve.wait_ge(pe_done[b], PE.after(name, i))
                nc.vector.tensor_tensor(z[b][:], psum[b][:], x[b][:], ALU.add).then_inc(dve_done[b], 1)

        def dve_segments(dve, DV, i, name_before, mask, values, sums, name):
            for b in S:
                if name_before == "psum":
                    pass
                elif name_before:
                    dve.wait_ge(dve_done[b], DV.after(name_before, i))
                nc.vector.tensor_tensor_scan(sums[b][:], mask[b][:], values[b][:], sums[b - 1][:, GR - 1:GR],
                                             ALU.mult, ALU.add).then_inc(dve_done[b], 1)

        def chain_sweep(dense):
            part = ExitStack()
            with part:
                name = "dense" if dense else "chain"
                xr, xT, hT, z, xb, x1, x2, x3 = tiles(part, name, "xr", "xT", "hT", "z", "xb", "x1", "x2", "x3")
                if dense:
                    sq, = tiles(part, name, "sq")
                    keep, = tiles(part, name, "keep", width=J)
                    found, = tiles(part, name, "found", width=J, dt=I32)
                else:
                    h1, h2 = tiles(part, name, "h1", "h2")
                    idx, = tiles(part, name, "idx", width=J, dt=I32)
                iters = DENSE_ITERS if dense else EDGE_ITERS
                tabs = [] if dense else ["h1_rows"]
                tabs2 = [] if dense else ["h2_rows"]
                PE = Steps(pe_done, ["xT", "upd_h", "upd_o", "x1T", "sage_h"] + tabs + ["sage_o", "x2T", "gcn_h"]
                           + tabs2 + ["gcn_o"] + (["sums"] if dense else []))
                AC = Steps(act_done, ["xT", "upd_h", "ln0_root", "ln1_root", "x1T", "sage_h"] + tabs
                           + ["ln2_root", "x2T", "gcn_h"] + tabs2 + ["ln3_root"] + (["squares", "ln4_root"] if dense else []))
                DV = Steps(dve_done, (["keep"] if dense else []) + ["z0"] + norm_dve("ln0") + ["ln0_w", "ln0_x"]
                           + norm_dve("ln1") + ["z2"] + norm_dve("ln2") + ["z3"] + norm_dve("ln3")
                           + (norm_dve("ln4") + ["sums"] if dense else []))
                PO = Steps(pool_done, ["xb"])
                LD = Steps(loaded, ["x", "found"], 16)
                IX = Steps(idx_loaded, ["idx"], 16)
                GA = Steps(gathered, [f"x{j}" for j in range(J)], 16)
                ST = Steps(stored, ["out"] if dense else ["x1", "h1", "x2", "h2", "x3"], 16)
                rows_in = (loaded, LD) if dense else (gathered, GA)

                def first_row(i, b):
                    if isinstance(i, int) and i == DENSE_ITERS - 1 and b == SLOTS - 1:
                        return N - GR
                    return at(i, b)

                last = DENSE_ITERS - 1
                block = part.enter_context(nc.Block())

                @block.sync
                def _(sp):
                    def load(i, b):
                        if dense:
                            sp.dma_start(xr[b][:], dram_rows(x, first_row(i, b))).then_inc(loaded[b], 16)
                            sp.dma_start(found[b][:], slot_of[bass.ds(first_row(i, b), GR), :]
                                         .rearrange("(p j) a -> p (j a)", j=J)).then_inc(loaded[b], 16)
                        else:
                            sp.dma_start(idx[b][:], dram_vec(src_gather_idx, at(i, b))).then_inc(idx_loaded[b], 16)

                    def store(i):
                        if dense:
                            for b in S:
                                wait_alone(sp, dve_done[b], DV.after("ln4_norm", i))
                                if isinstance(i, int) and i == last and b == SLOTS - 1:
                                    p0 = (DG * GR - N) // J
                                    sp.dma_start(dram_rows(out, N - (P - p0) * J, (P - p0) * J), z[b][p0:P, :])\
                                      .then_inc(stored[b], 16)
                                else:
                                    sp.dma_start(dram_rows(out, at(i, b)), z[b][:]).then_inc(stored[b], 16)
                            return
                        for t, ready, table_n in ((x1, (dve_done, DV, "ln1_norm"), X1), (h1, (act_done, AC, "h1_rows"), H1),
                                                  (x2, (dve_done, DV, "ln2_norm"), X2S), (h2, (act_done, AC, "h2_rows"), H2S),
                                                  (x3, (dve_done, DV, "ln3_norm"), X3)):
                            sems, steps, step = ready
                            for b in S:
                                wait_alone(sp, sems[b], steps.after(step, i))
                                sp.dma_start(dram_rows(table[table_n], at(i, b) + EP), t[b][:]).then_inc(stored[b], 16)

                    def free(i, b):
                        wait_alone(sp, dve_done[b], DV.all(i))
                        wait_alone(sp, stored[b], ST.all(i))

                    run_sync(sp, iters, load, store, free)

                @block.gpsimd
                def _(pool):
                    with pool.Fori(0, iters) as i:
                        for b in S:
                            if dense:
                                pool.wait_ge(loaded[b], LD.all(i))
                            else:
                                wait_alone(pool, idx_loaded[b], IX.all(i))
                                for j in range(J):
                                    gather(pool, rows(xr[b], j), idx[b], x, j, gathered[b])
                        for b in S:
                            if not dense:
                                pool.wait_ge(gathered[b], GA.all(i))
                            nc.gpsimd.tensor_tensor(xb[b][:], xr[b][:], ln_b[:], ALU.add).then_inc(pool_done[b], 1)

                @block.tensor
                def _(pe):
                    with pe.Fori(0, iters) as i:
                        for b in S:
                            pe.wait_ge(rows_in[0][b], rows_in[1].all(i))
                            pe_to_cols(b, xr[b]).then_inc(pe_done[b], 1)
                        for b in S:
                            pe.wait_ge(act_done[b], AC.after("xT", i))
                            pe_features(b, ("upd_x", xT[b])).then_inc(pe_done[b], 1)
                        for b in S:
                            pe.wait_ge(act_done[b], AC.after("upd_h", i))
                            pe_nodes(b, "upd_b2", ("upd_out", hT[b])).then_inc(pe_done[b], 1)
                        for b in S:
                            pe.wait_ge(dve_done[b], DV.after("ln1_norm", i))
                            pe_to_cols(b, x1[b]).then_inc(pe_done[b], 1)
                        for b in S:
                            pe.wait_ge(act_done[b], AC.after("x1T", i))
                            pe_features(b, ("sage1_r", xT[b])).then_inc(pe_done[b], 1)
                        if not dense:
                            for b in S:
                                pe.wait_ge(act_done[b], AC.after("sage_h", i))
                                pe_to_rows(b, hT[b]).then_inc(pe_done[b], 1)
                        for b in S:
                            pe.wait_ge(act_done[b], AC.after("sage_h" if dense else "h1_rows", i))
                            pe_nodes(b, "sage_b2", ("sage2_r", hT[b])).then_inc(pe_done[b], 1)
                        for b in S:
                            pe.wait_ge(dve_done[b], DV.after("ln2_norm", i))
                            pe_to_cols(b, x2[b]).then_inc(pe_done[b], 1)
                        for b in S:
                            pe.wait_ge(act_done[b], AC.after("x2T", i))
                            pe_features(b, ("gcn1", xT[b])).then_inc(pe_done[b], 1)
                        if not dense:
                            for b in S:
                                pe.wait_ge(act_done[b], AC.after("gcn_h", i))
                                pe_to_rows(b, hT[b]).then_inc(pe_done[b], 1)
                        for b in S:
                            pe.wait_ge(act_done[b], AC.after("gcn_h" if dense else "h2_rows", i))
                            pe_nodes(b, "gcn_b2", ("gcn2", hT[b])).then_inc(pe_done[b], 1)
                        if dense:
                            for b in S:
                                pe.wait_ge(act_done[b], AC.after("squares", i))
                                pe_sums(b, x3[b], sq[b], keep[b]).then_inc(pe_done[b], 1)

                @block.scalar
                def _(act):
                    with act.Fori(0, iters) as i:
                        act_copy(act, PE, "xT", i, xT)
                        act_copy(act, PE, "upd_h", i, hT, ACT.Relu, bias=colb["upd_b1"][:])
                        act_root(act, DV, "ln0", i)
                        act_root(act, DV, "ln1", i)
                        act_copy(act, PE, "x1T", i, xT)
                        act_copy(act, PE, "sage_h", i, hT, ACT.Relu, bias=colb["sage_b1"][:])
                        if not dense:
                            act_copy(act, PE, "h1_rows", i, h1)
                        act_root(act, DV, "ln2", i)
                        act_copy(act, PE, "x2T", i, xT)
                        act_copy(act, PE, "gcn_h", i, hT, ACT.Relu, bias=colb["gcn_b1"][:])
                        if not dense:
                            act_copy(act, PE, "h2_rows", i, h2)
                        act_root(act, DV, "ln3", i)
                        if dense:
                            for b in S:
                                act.wait_ge(dve_done[b], DV.after("ln3_norm", i))
                                nc.scalar.activation(sq[b][:], x3[b][:], ACT.Square).then_inc(act_done[b], 1)
                            act_root(act, DV, "ln4", i)

                @block.vector
                def _(dve):
                    def body(i):
                        if dense:
                            for b in S:
                                dve.wait_ge(loaded[b], LD.all(i))
                                if isinstance(i, int) and i == last and b == SLOTS - 1:
                                    nc.vector.tensor_scalar(keep[b][:], found[b][:], 0.0, last_group_keep[:],
                                                            ALU.is_lt, ALU.mult).then_inc(dve_done[b], 1)
                                else:
                                    nc.vector.tensor_scalar(keep[b][:], found[b][:], 0.0, None, ALU.is_lt)\
                                      .then_inc(dve_done[b], 1)
                        dve_residual(dve, PE, "upd_o", i, z, xr)
                        dve_stats(dve, DV, "ln0", i, z, "z0")
                        dve_norm(dve, DV, AC, "ln0", i, z, z)
                        dve_affine(dve, DV, i, z, xb, PO)
                        dve_stats(dve, DV, "ln1", i, z, "ln0_x")
                        dve_norm(dve, DV, AC, "ln1", i, z, x1)
                        dve_residual(dve, PE, "sage_o", i, z, x1)
                        dve_stats(dve, DV, "ln2", i, z, "z2")
                        dve_norm(dve, DV, AC, "ln2", i, z, x2)
                        dve_residual(dve, PE, "gcn_o", i, z, x2)
                        dve_stats(dve, DV, "ln3", i, z, "z3")
                        dve_norm(dve, DV, AC, "ln3", i, z, x3)
                        if dense:
                            dve_stats(dve, DV, "ln4", i, x3, "ln3_norm")
                            dve_norm(dve, DV, AC, "ln4", i, x3, z)
                            for b in S:
                                dve.wait_ge(pe_done[b], PE.after("sums", i))
                                nc.vector.tensor_tensor(bn_part[b][:], bn_part[b][:], psum[b][:, 0:2], ALU.add)\
                                  .then_inc(dve_done[b], 1)

                    if dense:
                        for b in S:
                            ins = nc.vector.memset(bn_part[b][:], 0.0)
                        link(dve, ins)
                    with dve.Fori(0, iters - 1) as i:
                        body(i)
                    body(iters - 1)

                for s in (PE, AC, DV, PO, ST) + ((LD,) if dense else (IX, GA)):
                    s.close(iters)

        def edge_message_sweep():
            part = ExitStack()
            with part:
                sr, tr, er, sT, tT, eT, agg, xb, mask = tiles(part, "msg", "sr", "tr", "er", "sT", "tT", "eT", "agg", "xb", "mask")
                s_idx, t_idx = tiles(part, "msg", "s_idx", "t_idx", width=J, dt=I32)
                z, x1 = sr, er
                PE = Steps(pe_done, ["sT", "tT", "eT", "msg_h", "msg", "upd_h", "upd_o"])
                AC = Steps(act_done, ["sT", "tT", "eT", "msg_h", "msg", "upd_h", "ln0_root", "ln1_root"])
                DV = Steps(dve_done, ["agg", "z0"] + norm_dve("ln0") + ["ln0_w", "ln0_x"] + norm_dve("ln1"))
                PO = Steps(pool_done, ["xb"])
                LD = Steps(loaded, ["edge", "mask"], 16)
                IX = Steps(idx_loaded, ["s", "t"], 16)
                GA = Steps(gathered, [f"{n}{j}" for n in "st" for j in range(J)], 16)
                ST = Steps(stored, ["x1"], 16)
                block = part.enter_context(nc.Block())

                @block.sync
                def _(sp):
                    def load(i, b):
                        sp.dma_start(s_idx[b][:], dram_vec(src_gather_idx, at(i, b))).then_inc(idx_loaded[b], 16)
                        sp.dma_start(t_idx[b][:], dram_vec(dst_gather_idx, at(i, b))).then_inc(idx_loaded[b], 16)
                        if isinstance(i, int) and at(i, b) + GR > E:
                            left = E - at(i, b)
                            sp.dma_start(er[b][0:left // J, :], dram_rows(edge_attr, at(i, b), left)).then_inc(loaded[b], 16)
                        else:
                            sp.dma_start(er[b][:], dram_rows(edge_attr, at(i, b))).then_inc(loaded[b], 16)
                        sp.dma_start(mask[b][:], edge_rows[bass.ds(i * SLOTS + b, 1), MASK, :]
                                     .rearrange("a c -> (a c)").partition_broadcast(P)).then_inc(loaded[b], 16)

                    def store(i):
                        for b in S:
                            wait_alone(sp, dve_done[b], DV.after("ln1_norm", i))
                            sp.dma_start(dram_rows(table[X1], at(i, b)), x1[b][:]).then_inc(stored[b], 16)

                    def free(i, b):
                        wait_alone(sp, stored[b], ST.all(i))

                    run_sync(sp, EDGE_ITERS, load, store, free)

                @block.gpsimd
                def _(pool):
                    with pool.Fori(0, EDGE_ITERS) as i:
                        for b in S:
                            wait_alone(pool, idx_loaded[b], IX.all(i))
                            for j in range(J):
                                gather(pool, rows(sr[b], j), s_idx[b], x, j, gathered[b])
                            for j in range(J):
                                gather(pool, rows(tr[b], j), t_idx[b], x, j, gathered[b])
                        for b in S:
                            pool.wait_ge(gathered[b], GA.all(i))
                            nc.gpsimd.tensor_tensor(xb[b][:], tr[b][:], ln_b[:], ALU.add).then_inc(pool_done[b], 1)

                @block.tensor
                def _(pe):
                    with pe.Fori(0, EDGE_ITERS) as i:
                        for b in S:
                            pe.wait_ge(gathered[b], GA.all(i))
                            pe_to_cols(b, sr[b]).then_inc(pe_done[b], 1)
                        for b in S:
                            pe.wait_ge(act_done[b], AC.after("sT", i))
                            pe_to_cols(b, tr[b]).then_inc(pe_done[b], 1)
                        for b in S:
                            pe.wait_ge(loaded[b], LD.all(i))
                            pe.wait_ge(act_done[b], AC.after("tT", i))
                            pe_to_cols(b, er[b]).then_inc(pe_done[b], 1)
                        for b in S:
                            pe.wait_ge(act_done[b], AC.after("eT", i))
                            pe_features(b, ("msg_src", sT[b]), ("msg_dst", tT[b]), ("msg_edge", eT[b])).then_inc(pe_done[b], 1)
                        for b in S:
                            pe.wait_ge(act_done[b], AC.after("msg_h", i))
                            pe_features(b, ("msg_out", sT[b])).then_inc(pe_done[b], 1)
                        for b in S:
                            pe.wait_ge(dve_done[b], DV.after("agg", i))
                            pe_features(b, ("upd_x", tT[b]), ("upd_agg", agg[b])).then_inc(pe_done[b], 1)
                        for b in S:
                            pe.wait_ge(act_done[b], AC.after("upd_h", i))
                            pe_nodes(b, "upd_b2", ("upd_out", sT[b])).then_inc(pe_done[b], 1)

                @block.scalar
                def _(act):
                    with act.Fori(0, EDGE_ITERS) as i:
                        act_copy(act, PE, "sT", i, sT)
                        act_copy(act, PE, "tT", i, tT)
                        act_copy(act, PE, "eT", i, eT)
                        act_copy(act, PE, "msg_h", i, sT, ACT.Relu, bias=colb["msg_b1"][:])
                        act_copy(act, PE, "msg", i, eT, ACT.Identity, bias=colb["msg_b2"][:])
                        act_copy(act, PE, "upd_h", i, sT, ACT.Relu, bias=colb["upd_b1"][:])
                        act_root(act, DV, "ln0", i)
                        act_root(act, DV, "ln1", i)

                @block.vector
                def _(dve):
                    link(dve, nc.vector.memset(agg[SLOTS - 1][:, GR - 1:GR], 0.0))
                    if_loaded = LD
                    with dve.Fori(0, EDGE_ITERS) as i:
                        for b in S:
                            dve.wait_ge(loaded[b], if_loaded.all(i))
                            dve.wait_ge(act_done[b], AC.after("msg", i))
                            if b:
                                dve.wait_ge(dve_done[b - 1], DV.after("agg", i))
                            nc.vector.tensor_tensor_scan(agg[b][:], mask[b][:], eT[b][:], agg[b - 1][:, GR - 1:GR],
                                                         ALU.mult, ALU.add).then_inc(dve_done[b], 1)
                        dve_residual(dve, PE, "upd_o", i, z, tr)
                        dve_stats(dve, DV, "ln0", i, z, "z0")
                        dve_norm(dve, DV, AC, "ln0", i, z, z)
                        dve_affine(dve, DV, i, z, xb, PO)
                        dve_stats(dve, DV, "ln1", i, z, "ln0_x")
                        dve_norm(dve, DV, AC, "ln1", i, z, x1)

                for s in (PE, AC, DV, PO, LD, IX, GA, ST):
                    s.close(EDGE_ITERS)

        def edge_sweep(stage):
            part = ExitStack()
            with part:
                name = f"edge{stage}"
                gcn = stage >= 3
                hidden = stage in (1, 3)
                sr, tr, tT, agg, v, y, yT = tiles(part, name, "sr", "tr", "tT", "agg", "v", "y", "yT")
                mask, scale = tiles(part, name, "mask", "scale")
                weight = tiles(part, name, "weight")[0] if gcn else None
                res = tiles(part, name, "res")[0] if not hidden else None
                dis_col = tiles(part, name, "dis_col", width=J)[0] if stage == 2 else None
                end_col = tiles(part, name, "end_col", width=J)[0] if stage == 4 else None
                o_idx = tiles(part, name, "o_idx", width=J, dt=I32)[0] if stage == 4 else None
                s_idx, = tiles(part, name, "s_idx", width=J, dt=I32)
                source, own = {1: (X1, X1), 2: (H1, H1), 3: (X2S, X2S), 4: (H2S, H2S)}[stage]
                PE = Steps(pe_done, ["sT", "tT"] + {
                    1: ["h", "rows"], 2: ["o"], 3: ["h", "rows"], 4: ["o", "sums"]}[stage])
                AC = Steps(act_done, {1: ["tT", "h", "rows"], 2: ["tT", "ln_root"], 3: ["h", "rows"],
                                      4: ["ln_root", "squares", "ln4_root"]}[stage])
                DV = Steps(dve_done, {
                    1: ["agg", "mean"],
                    2: ["agg", "mean", "z"] + norm_dve("ln") + ["by_dis"],
                    3: ["weighted", "agg", "self", "scaled", "h_scaled"],
                    4: ["weighted", "agg", "self", "scaled", "z"] + norm_dve("ln") + norm_dve("ln4") + ["sums"]}[stage])
                LD = Steps(loaded, ["t", "mask", "scale"] + (["weight"] if gcn else []) + (["res"] if not hidden else [])
                           + {2: ["dis_col"], 4: ["end_col"]}.get(stage, []), 16)
                IX = Steps(idx_loaded, ["s"] + (["o"] if stage == 4 else []), 16)
                GA = Steps(gathered, [f"s{j}" for j in range(J)], 16)
                ST = Steps(stored, {1: ["h1"], 2: ["x2", "x2s"], 3: ["h2s"], 4: ["x3"]}[stage], 16)
                SC = Steps(scattered, [f"out{j}" for j in range(J)], 16) if stage == 4 else None
                block = part.enter_context(nc.Block())

                @block.sync
                def _(sp):
                    def row_of_group(i, b, r):
                        return edge_rows[bass.ds(i * SLOTS + b, 1), r, :].rearrange("a c -> (a c)").partition_broadcast(P)

                    def load(i, b):
                        sp.dma_start(s_idx[b][:], dram_vec(src_row, at(i, b))).then_inc(idx_loaded[b], 16)
                        if stage == 4:
                            sp.dma_start(o_idx[b][:], dram_vec(dst_out_idx, at(i, b))).then_inc(idx_loaded[b], 16)
                        sp.dma_start(tr[b][:], dram_rows(table[own], at(i, b))).then_inc(loaded[b], 16)
                        sp.dma_start(mask[b][:], row_of_group(i, b, MASK)).then_inc(loaded[b], 16)
                        sp.dma_start(scale[b][:], row_of_group(i, b, DIS if gcn else INV)).then_inc(loaded[b], 16)
                        if gcn:
                            sp.dma_start(weight[b][:], row_of_group(i, b, EW)).then_inc(loaded[b], 16)
                        if not hidden:
                            sp.dma_start(res[b][:], dram_rows(table[X1] if stage == 2 else x2_plain, at(i, b)))\
                              .then_inc(loaded[b], 16)
                        if stage == 2:
                            sp.dma_start(dis_col[b][:], edge_rows[bass.ds(i * SLOTS + b, 1), DIS, :]
                                         .rearrange("a (p j) -> p (a j)", j=J)).then_inc(loaded[b], 16)
                        if stage == 4:
                            sp.dma_start(end_col[b][:], dram_vec(is_end, at(i, b))).then_inc(loaded[b], 16)

                    def store(i):
                        for b in S:
                            if hidden:
                                wait_alone(sp, act_done[b], AC.after("rows", i))
                                sp.dma_start(dram_rows(table[H1 if stage == 1 else H2S], at(i, b)), y[b][:])\
                                  .then_inc(stored[b], 16)
                            elif stage == 2:
                                wait_alone(sp, dve_done[b], DV.after("by_dis", i))
                                sp.dma_start(dram_rows(x2_plain, at(i, b)), y[b][:]).then_inc(stored[b], 16)
                                sp.dma_start(dram_rows(table[X2S], at(i, b)), sr[b][:]).then_inc(stored[b], 16)
                            else:
                                wait_alone(sp, dve_done[b], DV.after("ln_norm", i))
                                sp.dma_start(dram_rows(table[X3], at(i, b)), y[b][:]).then_inc(stored[b], 16)

                    def free(i, b):
                        wait_alone(sp, stored[b], ST.all(i))
                        if stage == 4:
                            wait_alone(sp, scattered[b], SC.all(i))
                            wait_alone(sp, dve_done[b], DV.all(i))

                    run_sync(sp, EDGE_ITERS, load, store, free)

                @block.gpsimd
                def _(pool):
                    with pool.Fori(0, EDGE_ITERS) as i:
                        for b in S:
                            wait_alone(pool, idx_loaded[b], IX.all(i))
                            for j in range(J):
                                gather(pool, rows(sr[b], j), s_idx[b], table[source], j, gathered[b])
                        if stage == 4:
                            for b in S:
                                wait_alone(pool, dve_done[b], DV.after("ln4_norm", i))
                                for j in range(J):
                                    scatter(pool, out, o_idx[b], rows(sr[b], j), j, scattered[b], limit=N - 1)

                @block.tensor
                def _(pe):
                    with pe.Fori(0, EDGE_ITERS) as i:
                        for b in S:
                            pe.wait_ge(gathered[b], GA.all(i))
                            pe_to_cols(b, sr[b]).then_inc(pe_done[b], 1)
                        for b in S:
                            pe.wait_ge(loaded[b], LD.all(i))
                            pe.wait_ge(dve_done[b], DV.after("weighted" if gcn else "agg", i))
                            pe_to_cols(b, tr[b]).then_inc(pe_done[b], 1)
                        for b in S:
                            pe.wait_ge(dve_done[b], DV.after("scaled" if gcn else "mean", i))
                            if not gcn:
                                pe.wait_ge(act_done[b], AC.after("tT", i))
                            if stage == 1:
                                ins = pe_features(b, ("sage1_l", v[b]), ("sage1_r", tT[b]))
                            elif stage == 2:
                                ins = pe_nodes(b, "sage_b2", ("sage2_l", v[b]), ("sage2_r", tT[b]))
                            elif stage == 3:
                                ins = pe_features(b, ("gcn1", v[b]))
                            else:
                                ins = pe_nodes(b, "gcn_b2", ("gcn2", v[b]))
                            ins.then_inc(pe_done[b], 1)
                        if hidden:
                            for b in S:
                                if gcn:
                                    pe.wait_ge(dve_done[b], DV.after("h_scaled", i))
                                else:
                                    pe.wait_ge(act_done[b], AC.after("h", i))
                                pe_to_rows(b, yT[b]).then_inc(pe_done[b], 1)
                        if stage == 4:
                            for b in S:
                                pe.wait_ge(act_done[b], AC.after("squares", i))
                                pe_sums(b, y[b], yT[b], end_col[b]).then_inc(pe_done[b], 1)

                @block.scalar
                def _(act):
                    with act.Fori(0, EDGE_ITERS) as i:
                        if not gcn:
                            act_copy(act, PE, "tT", i, tT)
                        if hidden:
                            act_copy(act, PE, "h", i, yT, ACT.Relu, bias=colb["gcn_b1" if gcn else "sage_b1"][:])
                            act_copy(act, PE, "rows", i, y)
                        else:
                            act_root(act, DV, "ln", i)
                        if stage == 4:
                            for b in S:
                                act.wait_ge(dve_done[b], DV.after("ln_norm", i))
                                nc.scalar.activation(yT[b][:], y[b][:], ACT.Square).then_inc(act_done[b], 1)
                            act_root(act, DV, "ln4", i)

                @block.vector
                def _(dve):
                    link(dve, nc.vector.memset(agg[SLOTS - 1][:, GR - 1:GR], 0.0))
                    with dve.Fori(0, EDGE_ITERS) as i:
                        if gcn:
                            for b in S:
                                dve.wait_ge(loaded[b], LD.all(i))
                                dve.wait_ge(pe_done[b], PE.after("sT", i))
                                nc.vector.tensor_tensor(v[b][:], psum[b][:], weight[b][:], ALU.mult).then_inc(dve_done[b], 1)
                        for b in S:
                            if gcn:
                                dve.wait_ge(dve_done[b], DV.after("weighted", i))
                            else:
                                dve.wait_ge(loaded[b], LD.all(i))
                                dve.wait_ge(pe_done[b], PE.after("sT", i))
                            if b:
                                dve.wait_ge(dve_done[b - 1], DV.after("agg", i))
                            nc.vector.tensor_tensor_scan(agg[b][:], mask[b][:], (v if gcn else psum)[b][:],
                                                         agg[b - 1][:, GR - 1:GR], ALU.mult, ALU.add)\
                              .then_inc(dve_done[b], 1)
                        if gcn:
                            for b in S:
                                dve.wait_ge(dve_done[b], DV.after("agg", i))
                                dve.wait_ge(pe_done[b], PE.after("tT", i))
                                nc.vector.tensor_tensor(v[b][:], psum[b][:], agg[b][:], ALU.add).then_inc(dve_done[b], 1)
                            for b in S:
                                dve.wait_ge(dve_done[b], DV.after("self", i))
                                nc.vector.tensor_tensor(v[b][:], v[b][:], scale[b][:], ALU.mult).then_inc(dve_done[b], 1)
                        else:
                            for b in S:
                                dve.wait_ge(dve_done[b], DV.after("agg", i))
                                nc.vector.tensor_tensor(v[b][:], agg[b][:], scale[b][:], ALU.mult).then_inc(dve_done[b], 1)
                        if stage == 3:
                            for b in S:
                                dve.wait_ge(act_done[b], AC.after("h", i))
                                nc.vector.tensor_tensor(yT[b][:], yT[b][:], scale[b][:], ALU.mult).then_inc(dve_done[b], 1)
                        if not hidden:
                            dve_residual(dve, PE, "o", i, tr, res)
                            dve_stats(dve, DV, "ln", i, tr, "z")
                            dve_norm(dve, DV, AC, "ln", i, tr, y)
                        if stage == 2:
                            for b in S:
                                dve.wait_ge(dve_done[b], DV.after("ln_norm", i))
                                for j in range(J):
                                    ins = nc.vector.tensor_scalar(rows(sr[b], j), rows(y[b], j), dis_col[b][:, j:j + 1],
                                                                  None, ALU.mult)
                                ins.then_inc(dve_done[b], 1)
                        if stage == 4:
                            dve_stats(dve, DV, "ln4", i, y, "ln_norm")
                            dve_norm(dve, DV, AC, "ln4", i, y, sr)
                            for b in S:
                                dve.wait_ge(pe_done[b], PE.after("sums", i))
                                nc.vector.tensor_tensor(bn_part[b][:], bn_part[b][:], psum[b][:, 0:2], ALU.add)\
                                  .then_inc(dve_done[b], 1)

                for s in (PE, AC, DV, LD, IX, GA, ST) + ((SC,) if SC else ()):
                    s.close(EDGE_ITERS)

        chain_sweep(dense=False)
        edge_message_sweep()
        for stage in (1, 2, 3):
            edge_sweep(stage)
        chain_sweep(dense=True)
        edge_sweep(4)

        with ExitStack() as part:
            mean, square, var = (part.enter_context(nc.sbuf_tensor(n, [P, 1], F32)) for n in ("bn_mean", "bn_square", "bn_var"))
            var_ready, root_ready = sem("var_ready"), sem("bn_root")
            block = part.enter_context(nc.Block())

            @block.vector
            def _(dve):
                for b in S:
                    link(dve, nc.vector.tensor_tensor(bn_sum[:], bn_sum[:], bn_part[b][:], ALU.add))
                nc.vector.tensor_scalar(mean[:], bn_sum[:, 0:1], 1.0 / N, None, ALU.mult)
                link(dve, nc.vector.tensor_scalar(var[:], bn_sum[:, 1:2], 1.0 / N, None, ALU.mult))
                link(dve, nc.vector.tensor_tensor(square[:], mean[:], mean[:], ALU.mult))
                nc.vector.tensor_tensor(var[:], var[:], square[:], ALU.subtract).then_inc(var_ready, 1)
                dve.wait_ge(root_ready, 1)
                link(dve, nc.vector.reciprocal(var[:], var[:]))
                link(dve, nc.vector.tensor_tensor(bn_a[:], colb["gamma"][:], var[:], ALU.mult))
                link(dve, nc.vector.tensor_tensor(square[:], mean[:], bn_a[:], ALU.mult))
                link(dve, nc.vector.tensor_tensor(bn_c[:], colb["beta"][:], square[:], ALU.subtract))

            @block.scalar
            def _(act):
                act.wait_ge(var_ready, 1)
                nc.scalar.activation(var[:], var[:], ACT.Sqrt, bias=eps[:]).then_inc(root_ready, 1)

        with ExitStack() as part:
            sr, dr, mask, xns, xnd, t1, t2, num, den = tiles(part, "att", "sr", "dr", "mask", "xns", "xnd", "t1", "t2", "num", "den")
            s_idx, d_idx, o_idx = tiles(part, "att", "s_idx", "d_idx", "o_idx", width=J, dt=I32)
            PE = Steps(pe_done, ["sT", "k1", "sum1", "dT", "k2", "sum2", "map"])
            AC = Steps(act_done, ["sT", "tanh1", "dT", "tanh2", "exp", "ln_root"])
            DV = Steps(dve_done, ["quad1", "quad2", "score", "leaky", "weighted", "num", "den", "inv", "attn", "z"]
                       + norm_dve("ln"))
            LD = Steps(loaded, ["mask"], 16)
            IX = Steps(idx_loaded, ["s", "d", "o"], 16)
            GA = Steps(gathered, [f"{n}{j}" for n in "sd" for j in range(J)], 16)
            SC = Steps(scattered, [f"out{j}" for j in range(J)], 16)
            block = part.enter_context(nc.Block())

            @block.sync
            def _(sp):
                def load(i, b):
                    for t, v in ((s_idx, sorted_src_row), (d_idx, sorted_dst_row), (o_idx, src_out_idx)):
                        sp.dma_start(t[b][:], dram_vec(v, at(i, b))).then_inc(idx_loaded[b], 16)
                    sp.dma_start(mask[b][:], sorted_mask[bass.ds(at(i, b), GR)].partition_broadcast(P)).then_inc(loaded[b], 16)

                def free(i, b):
                    wait_alone(sp, scattered[b], SC.all(i))

                run_sync(sp, EDGE_ITERS, load, lambda i: None, free)

            @block.gpsimd
            def _(pool):
                with pool.Fori(0, EDGE_ITERS) as i:
                    for b in S:
                        wait_alone(pool, idx_loaded[b], IX.all(i))
                        for t, idx in ((sr, s_idx), (dr, d_idx)):
                            for j in range(J):
                                gather(pool, rows(t[b], j), idx[b], table[X3], j, gathered[b])
                    for b in S:
                        wait_alone(pool, dve_done[b], DV.after("ln_norm", i))
                        for j in range(J):
                            scatter(pool, out, o_idx[b], rows(t2[b], j), j, scattered[b], limit=N - 1)

            @block.tensor
            def _(pe):
                with pe.Fori(0, EDGE_ITERS) as i:
                    for b in S:
                        pe.wait_ge(gathered[b], GA.all(i))
                        pe_to_cols(b, sr[b]).then_inc(pe_done[b], 1)
                    for b in S:
                        pe.wait_ge(act_done[b], AC.after("sT", i))
                        pe_features(b, ("k1", xns[b])).then_inc(pe_done[b], 1)
                    for b in S:
                        pe.wait_ge(dve_done[b], DV.after("quad1", i))
                        pe_features(b, ("ones", t1[b])).then_inc(pe_done[b], 1)
                    for b in S:
                        pe.wait_ge(act_done[b], AC.after("tanh1", i))
                        pe_to_cols(b, dr[b]).then_inc(pe_done[b], 1)
                    for b in S:
                        pe.wait_ge(act_done[b], AC.after("dT", i))
                        pe_features(b, ("k2", xnd[b])).then_inc(pe_done[b], 1)
                    for b in S:
                        pe.wait_ge(dve_done[b], DV.after("quad2", i))
                        pe_features(b, ("ones", t2[b])).then_inc(pe_done[b], 1)
                    for b in S:
                        pe.wait_ge(dve_done[b], DV.after("attn", i))
                        pe_nodes(b, None, ("map", xns[b])).then_inc(pe_done[b], 1)

            @block.scalar
            def _(act):
                with act.Fori(0, EDGE_ITERS) as i:
                    act_copy(act, PE, "sT", i, xns, ACT.Identity, scale=bn_a[:], bias=bn_c[:])
                    act_copy(act, PE, "sum1", i, t1, ACT.Tanh)
                    act_copy(act, PE, "dT", i, xnd, ACT.Identity, scale=bn_a[:], bias=bn_c[:])
                    act_copy(act, PE, "sum2", i, t2, ACT.Tanh)
                    for b in S:
                        act.wait_ge(dve_done[b], DV.after("leaky", i))
                        nc.scalar.activation(t1[b][:], t2[b][:], ACT.Exp).then_inc(act_done[b], 1)
                    act_root(act, DV, "ln", i)

            @block.vector
            def _(dve):
                nc.vector.memset(num[SLOTS - 1][:, GR - 1:GR], 0.0)
                link(dve, nc.vector.memset(den[SLOTS - 1][:, GR - 1:GR], 0.0))
                with dve.Fori(0, EDGE_ITERS) as i:
                    for b in S:
                        dve.wait_ge(pe_done[b], PE.after("k1", i))
                        nc.vector.tensor_tensor(t1[b][:], psum[b][:], xns[b][:], ALU.mult).then_inc(dve_done[b], 1)
                    for b in S:
                        dve.wait_ge(pe_done[b], PE.after("k2", i))
                        nc.vector.tensor_tensor(t2[b][:], psum[b][:], xnd[b][:], ALU.mult).then_inc(dve_done[b], 1)
                    for b in S:
                        dve.wait_ge(act_done[b], AC.after("tanh2", i))
                        nc.vector.tensor_tensor(t1[b][:], t1[b][:], t2[b][:], ALU.add).then_inc(dve_done[b], 1)
                    for b in S:
                        dve.wait_ge(dve_done[b], DV.after("score", i))
                        nc.vector.scalar_tensor_tensor(out=t2[b][:], in0=t1[b][:], scalar=0.01, in1=t1[b][:],
                                                       op0=ALU.mult, op1=ALU.max).then_inc(dve_done[b], 1)
                    for b in S:
                        dve.wait_ge(act_done[b], AC.after("exp", i))
                        nc.vector.tensor_tensor(xns[b][:], t1[b][:], xnd[b][:], ALU.mult).then_inc(dve_done[b], 1)
                    for b in S:
                        dve.wait_ge(loaded[b], LD.all(i))
                        dve.wait_ge(dve_done[b], DV.after("weighted", i))
                        if b:
                            dve.wait_ge(dve_done[b - 1], DV.after("num", i))
                        nc.vector.tensor_tensor_scan(num[b][:], mask[b][:], xns[b][:], num[b - 1][:, GR - 1:GR],
                                                     ALU.mult, ALU.add).then_inc(dve_done[b], 1)
                    for b in S:
                        if b:
                            dve.wait_ge(dve_done[b - 1], DV.after("den", i))
                        nc.vector.tensor_tensor_scan(den[b][:], mask[b][:], t1[b][:], den[b - 1][:, GR - 1:GR],
                                                     ALU.mult, ALU.add).then_inc(dve_done[b], 1)
                    for b in S:
                        dve.wait_ge(dve_done[b], DV.after("den", i))
                        nc.vector.reciprocal(t2[b][:], den[b][:]).then_inc(dve_done[b], 1)
                    for b in S:
                        dve.wait_ge(dve_done[b], DV.after("inv", i))
                        nc.vector.tensor_tensor(xns[b][:], num[b][:], t2[b][:], ALU.mult).then_inc(dve_done[b], 1)
                    for b in S:
                        dve.wait_ge(pe_done[b], PE.after("map", i))
                        nc.vector.scalar_tensor_tensor(out=dr[b][:], in0=psum[b][:], scalar=0.0, in1=sr[b][:],
                                                       op0=ALU.max, op1=ALU.add).then_inc(dve_done[b], 1)
                    dve_stats(dve, DV, "ln", i, dr, "z")
                    dve_norm(dve, DV, AC, "ln", i, dr, t2)
            for s in (PE, AC, DV, LD, IX, GA, SC):
                s.close(EDGE_ITERS)


_INS = ["x", "src", "dst", "edge_attr_128", "edge_weight",
        "L0_gnn_W1", "L0_gnn_b1", "L0_gnn_W2", "L0_gnn_b2", "L0_gnn_U1", "L0_gnn_ub1", "L0_gnn_U2", "L0_gnn_ub2",
        "L0_gnn_ln_w", "L0_gnn_ln_b",
        "L1_gnn_W1_l", "L1_gnn_b1", "L1_gnn_W1_r", "L1_gnn_W2_l", "L1_gnn_b2", "L1_gnn_W2_r",
        "L2_gnn_W1", "L2_gnn_b1", "L2_gnn_W2", "L2_gnn_b2",
        "L3_gnn_kernel", "L3_gnn_kernel1", "L3_gnn_kernel2", "L3_gnn_gamma", "L3_gnn_beta"]


def program(nc, a, out):
    w1, u1 = a["L0_gnn_W1"], a["L0_gnn_U1"]
    w = {
        "matrices": {
            "msg_src": w1[0:D, :], "msg_dst": w1[D:2 * D, :], "msg_edge": w1[2 * D:3 * D, :], "msg_out": a["L0_gnn_W2"],
            "upd_x": u1[0:D, :], "upd_agg": u1[D:2 * D, :], "upd_out": a["L0_gnn_U2"],
            "sage1_l": a["L1_gnn_W1_l"], "sage1_r": a["L1_gnn_W1_r"],
            "sage2_l": a["L1_gnn_W2_l"], "sage2_r": a["L1_gnn_W2_r"],
            "gcn1": a["L2_gnn_W1"], "gcn2": a["L2_gnn_W2"],
            "map": a["L3_gnn_kernel"], "k1": a["L3_gnn_kernel1"], "k2": a["L3_gnn_kernel2"]},
        "columns": {"msg_b1": a["L0_gnn_b1"], "msg_b2": a["L0_gnn_b2"], "upd_b1": a["L0_gnn_ub1"],
                    "sage_b1": a["L1_gnn_b1"], "gcn_b1": a["L2_gnn_b1"],
                    "gamma": a["L3_gnn_gamma"], "beta": a["L3_gnn_beta"]},
        "rows": {"upd_b2": a["L0_gnn_ub2"], "sage_b2": a["L1_gnn_b2"], "gcn_b2": a["L2_gnn_b2"]},
        "ln_w": a["L0_gnn_ln_w"], "ln_b": a["L0_gnn_ln_b"],
    }
    build(nc, a["x"], a["src"], a["dst"], a["edge_attr_128"], a["edge_weight"], w, out)


def kernel(**inputs):
    import numpy as _np
    import concourse.bacc as _bacc
    from concourse import mybir as _mybir
    from concourse.bass_utils import run_bass_kernel_spmd as _run

    nc = _bacc.Bacc("TRN2", target_bir_lowering=False, num_devices=1)
    arrays, args = {}, {}
    for name in _INS:
        a = _np.ascontiguousarray(inputs[name])
        arrays[f"in_{name}_dram"] = a
        args[name] = nc.dram_tensor(f"in_{name}_dram", a.shape, _mybir.dt.from_np(a.dtype), kind="ExternalInput").ap()
    out = nc.dram_tensor("out_0_dram", inputs["x"].shape, _mybir.dt.float32, kind="ExternalOutput").ap()
    program(nc, args, out)
    r = _run(nc, [arrays], core_ids=[0])
    return r.results[0]["out_0_dram"]
```

```python
from contextlib import ExitStack

import concourse.bass as bass
from concourse import mybir

ALU = mybir.AluOpType
ACT = mybir.ActivationFunctionType
AX = mybir.AxisListType
F32 = mybir.dt.float32
I32 = mybir.dt.int32
BF16 = mybir.dt.bfloat16

P = 128
D = 128
J = 4
GR = P * J
BANKS = 8
EPS = 1e-5


class Lane:

    KINDS = ("pe_done", "act_done", "dve_done", "pool_done", "loaded", "listed", "gathered", "scattered", "stored")

    def __init__(self, sem, n):
        self.sems = {kind: sem(f"{kind}{n}") for kind in self.KINDS}
        self.reached = {kind: 0 for kind in self.KINDS}


class Steps:

    def __init__(self, lanes, kind, names, unit=1):
        self.names, self.unit, self.lanes, self.kind = names, unit, lanes, kind
        self.base = [lane.reached[kind] for lane in lanes]
        self.sem = [lane.sems[kind] for lane in lanes]

    def done(self, name, i, b):
        n = len(self.names) * self.unit
        return self.sem[b], self.base[b] + (self.names.index(name) + 1) * self.unit + i * n

    def all(self, i, b):
        return self.done(self.names[-1], i, b)

    def close(self, b, iters):
        self.lanes[b].reached[self.kind] += iters * len(self.names) * self.unit


class Stream:

    def __init__(self, lanes, groups, chain, run, steps):
        self.slots, self.groups, self.chain, self.run, self.steps = len(lanes), groups, chain, run, steps

    def iters(self, b):
        return -(-(self.groups - b) // self.slots)


def timetable(engine, streams):
    order = []
    for n, s in enumerate(streams):
        whole = sum(time for _, _, time in s.chain)
        for b in range(s.slots):
            at = 0.0
            for m, (who, step, time) in enumerate(s.chain):
                place = at / whole + b / s.slots
                if who == engine:
                    order.append((place % 1.0, int(place), n, b, m, s, step))
                at += time
    order.sort(key=lambda x: x[:5])
    return [(back, s, b, step) for _, back, _, b, _, s, step in order]


def run_turns(eng, engine, streams):
    table = timetable(engine, streams)
    full = min(s.iters(b) for s in streams for b in range(s.slots)) - 1
    whole = max(s.iters(b) for s in streams for b in range(s.slots))

    def iteration(i):
        for back, s, b, step in table:
            k = i - back
            if not isinstance(i, int) or 0 <= k < s.iters(b):
                s.run[engine](eng, step, k, b)

    iteration(0)
    if table and full > 2:
        with eng.Fori(1, full) as i:
            iteration(i)
    for i in range(max(1, full) if full > 2 else 1, whole + 1):
        iteration(i)


def cols(t, j):
    return t.rearrange("f (p j) -> f j p", j=J)[:, j, :]


def rows(t, j):
    return t[:, j * D:(j + 1) * D]


def dram_rows(t, r, n=GR):
    return t[bass.ds(r, n), :].rearrange("(p j) f -> p (j f)", j=J)


def dram_vec(t, r, n=GR):
    return t[bass.ds(r, n)].rearrange("(p j) -> p j", j=J)


class K:
    pass


def build(nc, x, src, dst, edge_attr, edge_weight, w, out):
    N = x.shape[0]
    E = src.shape[0]
    EG = -(-E // GR)
    EP = EG * GR
    DG = -(-N // GR)
    QUARTERS = 4
    assert DG == QUARTERS * EG and EG <= P and x.shape[1] == D
    LO = 512
    PADNODE = -(-N // LO) * LO - 1
    DUMP = PADNODE + 1
    SLOTOF = DUMP + EP
    OOB = 1 << 20
    LO_CHUNKS = LO // P
    HI_CHUNKS = -(-((PADNODE // LO) + 1) // P)

    ctx = ExitStack()
    with ctx:
        k = K()

        def sb(name, shape, dt=F32):
            return ctx.enter_context(nc.sbuf_tensor(name, shape, dt))

        def sem(name):
            return ctx.enter_context(nc.semaphore(name))

        def dram(name, shape, dt=F32):
            return nc.dram_tensor(name, shape, dt).ap()

        table = [dram(f"table{n}", [2 * EP, D]) for n in range(5)]
        X1, H1, X2S, H2S, X3 = range(5)
        x2_plain = dram("x2_plain", [EP, D])
        slot_of = dram("slot_of", [SLOTOF, 1], I32)
        dst_pad = dram("dst_pad", [EP + 2], I32)
        src_pad = dram("src_pad", [EP], I32)
        ew_pad = dram("ew_pad", [EP])
        edge_rows = dram("edge_rows", [EG, 4, GR])
        INV, MASK, EW, DIS = range(4)
        is_end = dram("is_end", [EP])
        dst_slot_idx = dram("dst_slot_idx", [EP], I32)
        edge_id = dram("edge_id", [EP], I32)
        src_gather_idx = dram("src_gather_idx", [EP], I32)
        dst_gather_idx = dram("dst_gather_idx", [EP], I32)
        src_found = dram("src_found", [EP], I32)
        src_row = dram("src_row", [EP], I32)
        dst_out_idx = dram("dst_out_idx", [EP], I32)
        digit = [dram(f"digit{n}", [EP]) for n in range(2)]
        record = [dram(f"record{n}", [EP, 4], I32) for n in range(3)]
        sorted_src = dram("sorted_src", [EP + 2], I32)
        sorted_mask = dram("sorted_mask", [EP])
        sorted_src_row = dram("sorted_src_row", [EP], I32)
        sorted_dst_row = dram("sorted_dst_row", [EP], I32)
        src_out_idx = dram("src_out_idx", [EP], I32)

        lanes = [Lane(sem, n) for n in range(14)]
        const_ready = sem("const_ready")
        weights_in = sem("weights_in")
        bias_split = sem("bias_split")
        dve_link = sem("dve_link")
        fill_ready = sem("fill_ready")
        pads_written = sem("pads_written")
        block_in = sem("block_in")
        iota_ready = sem("iota_ready")
        tails_ready = sem("tails_ready")
        tails_row = sem("tails_row")
        carry_row = sem("carry_row")
        carry_col = sem("carry_col")
        act_line = sem("act_line")
        sqrt_in = sem("sqrt_in")
        vectors_ready = sem("vectors_ready")
        vectors_written = sem("vectors_written")
        totals_ready = sem("totals_ready")
        bases_ready = sem("bases_ready")
        weights_total = 16 * (len(w["matrices"]) + len(w["columns"]) + 2 * J + len(w["rows"]))
        count = {}

        ident = sb("ident", [P, P])
        ones = sb("ones", [P, P])
        before = sb("before", [P, P])
        iota_bin = sb("iota_bin", [P, LO_CHUNKS])
        earlier = sb("earlier", [P, J, GR], BF16)
        eps = sb("eps", [P, 1])
        last_group_keep = sb("last_group_keep", [P, 1])
        W = {n: sb(f"w_{n}", [P, D]) for n in (
            "msg_src", "msg_dst", "msg_edge", "msg_out", "upd_x", "upd_agg", "upd_out",
            "sage1_l", "sage1_r", "sage2_l", "sage2_r", "gcn1", "gcn2", "map", "k1", "k2")}
        colb = {n: sb(f"c_{n}", [P, 1]) for n in ("msg_b1", "msg_b2", "upd_b1", "sage_b1", "gcn_b1", "gamma", "beta")}
        ln_w = sb("ln_w", [P, GR])
        ln_b = sb("ln_b", [P, GR])
        bias_rows = {n: sb(f"r_{n}", [3, GR], BF16) for n in ("upd_b2", "sage_b2", "gcn_b2")}
        ones_bf = sb("ones_bf", [3, P], BF16)
        bn_sum = sb("bn_sum", [P, 2])
        bn_part = [sb(f"bn_part{n}", [P, 2]) for n in range(BANKS)]
        hist = sb("hist", [P, LO_CHUNKS, EG])
        first = sb("first", [P, LO_CHUNKS, EG])
        bn_a = sb("bn_a", [P, 1])
        bn_c = sb("bn_c", [P, 1])
        bank = [ctx.enter_context(nc.psum_tensor(f"bank{b}", [P, GR], F32)) for b in range(BANKS)]
        spare = bank[BANKS - 1]


        def reach(s, by=1):
            count[s] = count.get(s, 0) + by
            return count[s]

        def link(dve, ins):
            ins.then_inc(dve_link, 1)
            dve.wait_ge(dve_link, reach(dve_link))

        lo_pad = EP - E
        with (
            nc.sbuf_tensor("fill", [1, 2 * P], I32) as fill,
            nc.sbuf_tensor("fill_weight", [1, P], F32) as fill_weight,
            nc.sbuf_tensor("nothing", [P, SLOTOF // P], I32) as nothing,
            nc.sbuf_tensor("bias_in", [3, 3, D], F32) as bias_in,
            nc.sbuf_tensor("bias_tmp", [3, 4, D], F32) as bias_tmp,
            nc.sbuf_tensor("bias_hi", [3, D], BF16) as bias_hi,
            nc.sbuf_tensor("centred", [P, D], F32) as centred,
            nc.sbuf_tensor("row_mean", [P, 1], F32) as row_mean,
            nc.Block() as block,
        ):
            assert SLOTOF % P == 0

            @block.gpsimd
            def _(pool):
                nc.gpsimd.memset(ident[:], 0.0).then_inc(const_ready, 1)
                nc.gpsimd.memset(ones[:], 1.0).then_inc(const_ready, 1)
                nc.gpsimd.memset(earlier[:], 1.0).then_inc(const_ready, 1)
                nc.gpsimd.memset(last_group_keep[:], 1.0).then_inc(const_ready, 1)
                pool.wait_ge(const_ready, 4)
                pool.affine_select(out=ident[:], in_=ident[:], compare_op=ALU.not_equal, fill=1.0, base=0,
                                   pattern=[[-1, P]], channel_multiplier=1).then_inc(const_ready, 1)
                pool.affine_select(out=before[:], in_=ones[:], compare_op=ALU.is_gt, fill=0.0, base=0,
                                   pattern=[[1, P]], channel_multiplier=-1).then_inc(const_ready, 1)
                pool.affine_select(out=earlier[:], in_=earlier[:], compare_op=ALU.is_gt, fill=0.0, base=0,
                                   pattern=[[1, J], [-1, GR]], channel_multiplier=J).then_inc(const_ready, 1)
                pool.affine_select(out=last_group_keep[:], in_=last_group_keep[:], compare_op=ALU.is_ge, fill=0.0,
                                   base=-((DG * GR - N) // J), pattern=[[0, 1]],
                                   channel_multiplier=1).then_inc(const_ready, 1)
                pool.iota(iota_bin[:], pattern=[[P, LO_CHUNKS]], base=0, channel_multiplier=1,
                          allow_small_or_imprecise_dtypes=True).then_inc(const_ready, 1)

            @block.vector
            def _(dve):
                nc.vector.memset(fill[0:1, 0:P], -1)
                nc.vector.memset(fill[0:1, P:2 * P], PADNODE)
                nc.vector.memset(fill_weight[:], 0.0)
                nc.vector.memset(nothing[:], -1).then_inc(fill_ready, 1)
                nc.vector.memset(ones_bf[:], 1.0)
                nc.vector.memset(eps[:], EPS)
                nc.vector.memset(bn_sum[:], 0.0)
                for t in bn_part:
                    nc.vector.memset(t[:], 0.0)
                dve.wait_ge(const_ready, 9)
                dve.wait_ge(weights_in, weights_total)
                for name in ("sage2_l", "sage2_r", "gcn2"):
                    link(dve, nc.vector.tensor_scalar(centred[:], W[name][:], 1.0 / D, None, ALU.mult, ALU.add,
                                                      accum_out=row_mean[:]))
                    link(dve, nc.vector.tensor_scalar(W[name][:], W[name][:], row_mean[:], None, ALU.subtract))
                for name in ("sage_b2", "gcn_b2"):
                    bias = bias_in[:, list(bias_rows).index(name), :]
                    link(dve, nc.vector.tensor_scalar(centred[0:3, :], bias, 1.0 / D, None, ALU.mult, ALU.add,
                                                      accum_out=row_mean[0:3, :]))
                    link(dve, nc.vector.tensor_scalar(bias, bias, row_mean[0:3, :], None, ALU.subtract))
                for n, name in enumerate(bias_rows):
                    whole = bias_in[:, n, :]
                    for part in range(3):
                        rest = whole if part == 0 else bias_tmp[:, part - 1, :]
                        link(dve, nc.vector.tensor_copy(bias_hi[:], rest))
                        if part < 2:
                            nc.vector.tensor_tensor(bias_tmp[:, part, :], rest, bias_hi[:], ALU.subtract)
                        mine = ident[0:3, part:part + 1]
                        if part == 0:
                            link(dve, nc.vector.tensor_scalar(bias_tmp[:, 3, :], bias_hi[:], mine, None, ALU.mult))
                        else:
                            link(dve, nc.vector.scalar_tensor_tensor(out=bias_tmp[:, 3, :], in0=bias_hi[:], scalar=mine,
                                                                     in1=bias_tmp[:, 3, :], op0=ALU.mult, op1=ALU.add))
                    for j in range(J):
                        link(dve, nc.vector.tensor_copy(bias_rows[name][:, j * D:(j + 1) * D], bias_tmp[:, 3, :]))

            @block.sync
            def _(sp):
                for name, source in w["matrices"].items():
                    sp.dma_start(W[name][:], source).then_inc(weights_in, 16)
                for name, source in w["columns"].items():
                    sp.dma_start(colb[name][:], source.rearrange("(p a) -> p a", a=1)).then_inc(weights_in, 16)
                for j in range(J):
                    sp.dma_start(ln_w[:, j * D:(j + 1) * D], w["ln_w"].partition_broadcast(P)).then_inc(weights_in, 16)
                    sp.dma_start(ln_b[:, j * D:(j + 1) * D], w["ln_b"].partition_broadcast(P)).then_inc(weights_in, 16)
                for n, name in enumerate(bias_rows):
                    sp.dma_start(bias_in[:, n, :], w["rows"][name].partition_broadcast(3)).then_inc(weights_in, 16)
                sp.dma_start(dst_pad[1:1 + E], dst).then_inc(pads_written, 16)
                sp.dma_start(src_pad[0:E], src).then_inc(pads_written, 16)
                sp.dma_start(ew_pad[0:E], edge_weight).then_inc(pads_written, 16)
                sp.wait_ge(fill_ready, 1)
                def as_row(v, first, n):
                    return v[first:first + n].rearrange("(a n) -> a n", a=1)

                minus_one = fill[0:1, 0:1]
                sp.dma_start(as_row(dst_pad, 0, 1), minus_one).then_inc(pads_written, 16)
                sp.dma_start(as_row(dst_pad, 1 + E, lo_pad), fill[0:1, P:P + lo_pad]).then_inc(pads_written, 16)
                sp.dma_start(as_row(dst_pad, 1 + EP, 1), minus_one).then_inc(pads_written, 16)
                sp.dma_start(as_row(sorted_src, 0, 1), minus_one).then_inc(pads_written, 16)
                sp.dma_start(as_row(sorted_src, 1 + EP, 1), minus_one).then_inc(pads_written, 16)
                sp.dma_start(as_row(src_pad, E, lo_pad), fill[0:1, P:P + lo_pad]).then_inc(pads_written, 16)
                sp.dma_start(as_row(ew_pad, E, lo_pad), fill_weight[0:1, 0:lo_pad]).then_inc(pads_written, 16)
                sp.dma_start(slot_of.rearrange("(p n) a -> p (n a)", p=P), nothing[:]).then_inc(pads_written, 16)
                sp.wait_ge(pads_written, 11 * 16)
                sp.wait_ge(weights_in, weights_total)

        def block_view(v, first=0):
            return v[first:first + EP].rearrange("(g c) -> g c", g=EG)

        with ExitStack() as part:
            def tile(name, dt=F32, width=GR):
                return part.enter_context(nc.sbuf_tensor(name, [EG, width], dt))

            dst_i, prev_i, next_i, src_i = (tile(n, I32) for n in ("dst_i", "prev_i", "next_i", "src_i"))
            weight = tile("weight")
            edge_i = tile("edge_i", I32)
            edge_f, mask, go_on, end, zero, one_f = (tile(n) for n in ("edge_f", "mask", "go_on", "end", "zero", "one_f"))
            local = [tile(f"local{n}") for n in range(3)]
            runs = [tile(f"runs{n}") for n in range(2)]
            total = [tile(f"total{n}") for n in range(3)]
            tmp, tmp2 = tile("tmp"), tile("tmp2")
            int_total = tile("int_total", I32)
            int_out = [tile(f"int_out{n}", I32) for n in range(4)]
            tail_rows = part.enter_context(nc.sbuf_tensor("tail_rows", [1, 2, EG], F32))
            carry = part.enter_context(nc.sbuf_tensor("carry", [1, EG], F32))
            sums = part.enter_context(nc.sbuf_tensor("sums", [1, EG], F32))
            low_i = tile("low_i", I32)
            low_f = tile("low_f")
            block = part.enter_context(nc.Block())

            scans = [(0, 0, GR - 1), (1, 0, GR - 1), (2, 1, 0)]

            @block.sync
            def _(sp):
                for t, v, first in ((dst_i, dst_pad, 1), (prev_i, dst_pad, 0), (next_i, dst_pad, 2),
                                    (src_i, src_pad, 0), (weight, ew_pad, 0)):
                    sp.dma_start(t[:], block_view(v, first)).then_inc(block_in, 16)
                sp.wait_ge(vectors_ready, 1)
                for r, t in ((INV, total[0]), (MASK, mask), (EW, weight), (DIS, total[1])):
                    sp.dma_start(edge_rows[:, r, :], t[:]).then_inc(vectors_written, 16)
                sp.dma_start(block_view(is_end), end[:]).then_inc(vectors_written, 16)
                sp.dma_start(block_view(edge_id), edge_i[:]).then_inc(vectors_written, 16)
                for v, t in zip((dst_slot_idx, dst_gather_idx, src_gather_idx, dst_out_idx), int_out):
                    sp.dma_start(block_view(v), t[:]).then_inc(vectors_written, 16)
                sp.dma_start(block_view(sorted_dst_row), int_total[:]).then_inc(vectors_written, 16)
                sp.dma_start(block_view(digit[0]), low_f[:]).then_inc(vectors_written, 16)
                sp.wait_ge(vectors_written, 12 * 16)

            @block.gpsimd
            def _(pool):
                pool.iota(edge_i[:], pattern=[[1, GR]], base=0, channel_multiplier=GR).then_inc(iota_ready, 1)

            @block.tensor
            def _(pe):
                for n, (v, m, last) in enumerate(scans):
                    pe.wait_ge(tails_ready, n + 1)
                    nc.tensor.matmul(spare[0:1, 0:EG], local[v][:, last:last + 1], ident[0:EG, 0:EG], start=True, stop=True)
                    nc.tensor.matmul(spare[0:1, P:P + EG], runs[m][:, last:last + 1], ident[0:EG, 0:EG],
                                     start=True, stop=True).then_inc(tails_row, 1)
                    pe.wait_ge(carry_row, n + 1)
                    nc.tensor.matmul(spare[0:EG, 2 * P:2 * P + 1], carry[0:1, :], ones[0:1, 0:1],
                                     start=True, stop=True).then_inc(carry_col, 1)

            @block.scalar
            def _(act):
                act.wait_ge(sqrt_in, 1)
                nc.scalar.activation(tmp2[:], tmp[:], ACT.Sqrt).then_inc(act_line, 1)

            @block.vector
            def _(dve):
                nc.vector.memset(zero[:], 0.0)
                link(dve, nc.vector.memset(one_f[:], 1.0))
                dve.wait_ge(block_in, 5 * 16)
                dve.wait_ge(iota_ready, 1)
                nc.vector.tensor_copy(edge_f[:], edge_i[:])
                nc.vector.tensor_tensor(mask[:], dst_i[:], prev_i[:], ALU.is_equal)
                nc.vector.tensor_tensor(go_on[:], dst_i[:], next_i[:], ALU.is_equal)
                link(dve, nc.vector.tensor_tensor(end[:], dst_i[:], next_i[:], ALU.not_equal))
                link(dve, nc.vector.tensor_tensor(tmp[:], edge_f[:], end[:], ALU.mult))
                nc.vector.tensor_tensor_scan(local[0][:], mask[:], one_f[:], 0.0, ALU.mult, ALU.add)
                nc.vector.tensor_tensor_scan(local[1][:], mask[:], weight[:], 0.0, ALU.mult, ALU.add)
                nc.vector.tensor_tensor_scan(local[2][:, ::-1], go_on[:, ::-1], tmp[:, ::-1], 0.0, ALU.mult, ALU.add)
                nc.vector.tensor_tensor_scan(runs[0][:], mask[:], zero[:], 1.0, ALU.mult, ALU.add)
                link(dve, nc.vector.tensor_tensor_scan(runs[1][:, ::-1], go_on[:, ::-1], zero[:, ::-1], 1.0, ALU.mult, ALU.add))
                for n, (v, m, last) in enumerate(scans):
                    nc.vector.memset(carry[:], 0.0).then_inc(tails_ready, 1)
                    dve.wait_ge(tails_row, n + 1)
                    nc.vector.tensor_copy(tail_rows[0:1, 0, :], spare[0:1, 0:EG])
                    link(dve, nc.vector.tensor_copy(tail_rows[0:1, 1, :], spare[0:1, P:P + EG]))
                    if last:
                        link(dve, nc.vector.tensor_tensor_scan(sums[:], tail_rows[0:1, 1, :], tail_rows[0:1, 0, :], 0.0,
                                                               ALU.mult, ALU.add))
                        nc.vector.tensor_copy(carry[0:1, 1:EG], sums[0:1, 0:EG - 1]).then_inc(carry_row, 1)
                    else:
                        link(dve, nc.vector.tensor_tensor_scan(sums[0:1, ::-1], tail_rows[0:1, 1, ::-1],
                                                               tail_rows[0:1, 0, ::-1], 0.0, ALU.mult, ALU.add))
                        nc.vector.tensor_copy(carry[0:1, 0:EG - 1], sums[0:1, 1:EG]).then_inc(carry_row, 1)
                    dve.wait_ge(carry_col, n + 1)
                    link(dve, nc.vector.scalar_tensor_tensor(out=total[v][:], in0=runs[m][:],
                                                             scalar=spare[0:EG, 2 * P:2 * P + 1],
                                                             in1=local[v][:], op0=ALU.mult, op1=ALU.add))
                nc.vector.tensor_copy(int_total[:], total[2][:])
                link(dve, nc.vector.tensor_scalar(low_i[:], src_i[:], LO - 1, None, ALU.bitwise_and))
                nc.vector.tensor_copy(low_f[:], low_i[:])
                link(dve, nc.vector.tensor_scalar(total[0][:], total[0][:], 1.0, None, ALU.max))
                link(dve, nc.vector.reciprocal(total[0][:], total[0][:]))
                link(dve, nc.vector.tensor_scalar(total[1][:], total[1][:], 1.0, None, ALU.add))
                nc.vector.tensor_scalar(tmp[:], total[1][:], 1e-12, None, ALU.max).then_inc(sqrt_in, 1)
                dve.wait_ge(act_line, 1)
                link(dve, nc.vector.reciprocal(tmp2[:], tmp2[:]))
                link(dve, nc.vector.scalar_tensor_tensor(out=total[1][:], in0=total[1][:], scalar=0.0, in1=tmp2[:],
                                                         op0=ALU.is_gt, op1=ALU.mult))
                link(dve, nc.vector.tensor_scalar(tmp[:], edge_f[:], float(DUMP), None, ALU.add))
                link(dve, nc.vector.tensor_tensor(tmp2[:], dst_i[:], tmp[:], ALU.subtract))
                link(dve, nc.vector.tensor_tensor(tmp2[:], tmp2[:], end[:], ALU.mult))
                nc.vector.tensor_tensor(int_out[0][:], tmp2[:], tmp[:], ALU.add)
                nc.vector.tensor_scalar(int_out[1][:], dst_i[:], float(N - 1), None, ALU.min)
                link(dve, nc.vector.tensor_scalar(int_out[2][:], src_i[:], float(N - 1), None, ALU.min))
                link(dve, nc.vector.tensor_scalar(tmp2[:], dst_i[:], float(N), None, ALU.is_lt))
                link(dve, nc.vector.tensor_tensor(tmp2[:], tmp2[:], end[:], ALU.mult))
                link(dve, nc.vector.tensor_scalar(tmp[:], dst_i[:], float(-OOB), None, ALU.add))
                link(dve, nc.vector.tensor_tensor(tmp[:], tmp[:], tmp2[:], ALU.mult))
                nc.vector.tensor_scalar(int_out[3][:], tmp[:], float(OOB), None, ALU.add).then_inc(vectors_ready, 1)


        def wait_alone(eng, s, value):
            eng.wait_ge(s, value)
            eng.nop(nofuse=True)

        def gather(pool, rows_out, idx, source, j, s):
            pool.indirect_dma_start(out=rows_out, out_offset=None, in_=source,
                                    in_offset=bass.IndirectOffsetOnAxis(ap=idx[:, j:j + 1], axis=0)).then_inc(s, 16)

        def scatter(pool, target, idx, rows_in, j, s, limit=None):
            more = {} if limit is None else {"bounds_check": limit, "oob_is_err": False}
            pool.indirect_dma_start(out=target, out_offset=bass.IndirectOffsetOnAxis(ap=idx[:, j:j + 1], axis=0),
                                    in_=rows_in, in_offset=None, **more).then_inc(s, 16)

        def tiles(part, name, slots, *names, shape=(GR,), dt=F32):
            return [[part.enter_context(nc.sbuf_tensor(f"{name}_{n}{b}", [P, *shape], dt)) for b in range(slots)]
                    for n in names]

        def to_cols(target, source):
            for j in range(J):
                ins = nc.tensor.transpose(cols(target[:], j), rows(source, j), ident[:])
            return ins

        def to_rows(target, source):
            for j in range(J):
                ins = nc.tensor.transpose(rows(target, j), cols(source[:], j), ident[:])
            return ins

        def features(target, *terms):
            for n, (weight, xT) in enumerate(terms):
                ins = nc.tensor.matmul(target[:], weight[:], xT[:], start=(n == 0), stop=(n == len(terms) - 1))
            return ins

        def nodes(target, bias, *terms):
            if bias:
                nc.tensor.matmul(target[:], ones_bf[:], bias_rows[bias][:], start=True, stop=False)
            for j in range(J):
                for n, (weight, xT) in enumerate(terms):
                    last = n == len(terms) - 1 and (not bias or j == J - 1)
                    ins = nc.tensor.matmul(rows(target, j), cols(xT[:], j), weight[:],
                                           start=(not bias and n == 0), stop=last)
            return ins

        def feature_sums(target, x3, keep, squares, keep_squares):
            for c, (t, weight) in enumerate(((x3, keep), (squares, keep_squares))):
                for j in range(J):
                    ins = nc.tensor.matmul(target[:, c:c + 1], rows(t, j), weight[:, j:j + 1],
                                           start=(j == 0), stop=(j == J - 1))
            return ins

        def row_stats(stats, source):
            for j in range(J):
                ins = nc.vector.bn_stats(stats[:, j, :], rows(source, j))
            return ins

        def row_moments(moments, stats):
            for j in range(J):
                ins = nc.vector.bn_aggr(moments[:, j, :], stats[:, j, :])
            return ins

        def norm_rows(target, source, moments, inv):
            for j in range(J):
                ins = nc.vector.tensor_scalar(rows(target, j), rows(source, j), moments[:, j, 0:1], inv[:, j:j + 1],
                                              ALU.subtract, ALU.mult)
            return ins

        def scale_rows(target, source, by):
            return nc.vector.tensor_tensor(target[:].rearrange("p (j f) -> p j f", j=J),
                                           source[:].rearrange("p (j f) -> p j f", j=J),
                                           by[:].unsqueeze(2).to_broadcast([P, J, D]), ALU.mult)

        def act_scale_rows(target, source, by):
            for j in range(J):
                ins = nc.scalar.activation(rows(target, j), rows(source, j), ACT.Copy, scale=by[:, j:j + 1])
            return ins

        def row_squares(squares, source, sums):
            for j in range(J):
                ins = nc.scalar.activation(rows(squares, j), rows(source, j), ACT.Square, accum_out=sums[:, j:j + 1])
            return ins

        def root_of(target, variance):
            return nc.scalar.activation(target[:], variance, ACT.Sqrt, bias=eps[:])

        def root_of_sums(target, sums):
            return nc.scalar.activation(target[:], sums[:], ACT.Sqrt, bias=eps[:], scale=1.0 / D)

        def sweep(*streams):
            with nc.Block() as block:
                @block.sync
                def _(sp):
                    run_turns(sp, "sp", streams)
                    for s in streams:
                        for b in range(s.slots):
                            s.run["free"](sp, s.iters(b) - 1, b)

                @block.gpsimd
                def _(pool):
                    run_turns(pool, "pool", streams)

                @block.tensor
                def _(pe):
                    run_turns(pe, "pe", streams)

                @block.scalar
                def _(act):
                    run_turns(act, "act", streams)

                @block.vector
                def _(dve):
                    run_turns(dve, "dve", streams)
            for s in streams:
                for b in range(s.slots):
                    for steps in s.steps:
                        steps.close(b, s.iters(b))

        def group_row(slots, k, b):
            return k * (slots * GR) + b * GR

        def is_first(k):
            return isinstance(k, int) and k == 0

        def start_sums(sums):
            with nc.Block() as block:
                @block.vector
                def _(dve):
                    for t in sums:
                        link(dve, nc.vector.memset(t[-1][:, GR - 1:GR], 0.0))

        def carried(dve, DV, step, k, b, slots):
            if b:
                dve.wait_ge(*DV.done(step, k, b - 1))
            elif not is_first(k):
                dve.wait_ge(*DV.done(step, k - 1, slots - 1))

        def slot_of_stream(part, lanes):
            slots = len(lanes)
            idx, val = tiles(part, "ends", slots, "idx", "val", shape=(J,), dt=I32)
            IX = Steps(lanes, "listed", ["idx", "val"], 16)
            SC = Steps(lanes, "scattered", [f"slot{j}" for j in range(J)], 16)

            def free(sp, k, b):
                wait_alone(sp, *SC.all(k, b))

            def sp_part(sp, step, k, b):
                if not is_first(k):
                    free(sp, k - 1, b)
                row = group_row(slots, k, b)
                sp.dma_start(idx[b][:], dram_vec(dst_slot_idx, row)).then_inc(IX.sem[b], 16)
                sp.dma_start(val[b][:], dram_vec(edge_id, row)).then_inc(IX.sem[b], 16)

            def pool_part(pool, step, k, b):
                wait_alone(pool, *IX.all(k, b))
                for j in range(J):
                    scatter(pool, slot_of, idx[b], val[b][:, j:j + 1], j, SC.sem[b])

            return Stream(lanes, EG, [("sp", "load", 3), ("pool", "scatter", 6)],
                          {"sp": sp_part, "pool": pool_part, "free": free}, (IX, SC))

        def src_found_stream(part, lanes):
            slots = len(lanes)
            idx, val = tiles(part, "own_end", slots, "idx", "val", shape=(J,), dt=I32)
            IX = Steps(lanes, "listed", ["idx"], 16)
            GA = Steps(lanes, "gathered", [f"slot{j}" for j in range(J)], 16)
            ST = Steps(lanes, "stored", ["found"], 16)

            def free(sp, k, b):
                wait_alone(sp, *ST.all(k, b))

            def sp_part(sp, step, k, b):
                row = group_row(slots, k, b)
                if step == "load":
                    if not is_first(k):
                        free(sp, k - 1, b)
                    sp.dma_start(idx[b][:], dram_vec(src_pad, row)).then_inc(IX.sem[b], 16)
                elif step == "store":
                    wait_alone(sp, *GA.all(k, b))
                    sp.dma_start(dram_vec(src_found, row), val[b][:]).then_inc(ST.sem[b], 16)

            def pool_part(pool, step, k, b):
                wait_alone(pool, *IX.all(k, b))
                for j in range(J):
                    gather(pool, val[b][:, j:j + 1], idx[b], slot_of, j, GA.sem[b])

            return Stream(lanes, EG, [("sp", "load", 3), ("pool", "gather", 8), ("sp", "store", 3)],
                          {"sp": sp_part, "pool": pool_part, "free": free}, (IX, GA, ST))

        def load_digits(sp, n, dig, row, s):
            sp.dma_start(dig[:], digit[n][bass.ds(row, GR)].partition_broadcast(P)).then_inc(s, 16)

        def hist_stream(part, lanes, n, chunks):
            slots = len(lanes)
            dig, hot = tiles(part, f"hist{n}", slots, "dig", "hot")
            LD = Steps(lanes, "loaded", ["digits"], 16)
            DV = Steps(lanes, "dve_done", [f"count{c}" for c in range(chunks)])

            def free(sp, k, b):
                wait_alone(sp, *DV.all(k, b))

            def sp_part(sp, step, k, b):
                if not is_first(k):
                    free(sp, k - 1, b)
                load_digits(sp, n, dig[b], group_row(slots, k, b), LD.sem[b])

            def dve_part(dve, step, k, b):
                c = int(step[-1])
                if c == 0:
                    dve.wait_ge(*LD.all(k, b))
                else:
                    dve.wait_ge(*DV.done(f"count{c - 1}", k, b))
                nc.vector.tensor_scalar(hot[b][:], dig[b][:], iota_bin[:, c:c + 1], None, ALU.is_equal, ALU.add,
                                        accum_out=hist[:, c, bass.ds(k * slots + b, 1)]).then_inc(DV.sem[b], 1)

            return Stream(lanes, EG, [("sp", "load", 4)] + [("dve", f"count{c}", 2) for c in range(chunks)],
                          {"sp": sp_part, "dve": dve_part, "free": free}, (LD, DV))

        def bin_bases(n, chunks):
            with ExitStack() as part:
                sums = part.enter_context(nc.sbuf_tensor(f"bin_sums{n}", [P, chunks, EG], F32))
                ones_g = part.enter_context(nc.sbuf_tensor(f"ones_g{n}", [P, EG], F32))
                lower = part.enter_context(nc.sbuf_tensor(f"lower{n}", [P, chunks], F32))
                totals = part.enter_context(nc.sbuf_tensor(f"totals{n}", [P, chunks], F32))
                block = part.enter_context(nc.Block())

                @block.vector
                def _(dve):
                    link(dve, nc.vector.memset(ones_g[:], 1.0))
                    for c in range(chunks):
                        link(dve, nc.vector.tensor_tensor_scan(sums[:, c, :], ones_g[:], hist[:, c, :], 0.0,
                                                               ALU.mult, ALU.add))
                        link(dve, nc.vector.tensor_tensor(first[:, c, :], sums[:, c, :], hist[:, c, :], ALU.subtract))
                    link(dve, nc.vector.memset(lower[:], 0.0))
                    for c in range(1, chunks):
                        link(dve, nc.vector.tensor_tensor(lower[:, c:c + 1], lower[:, c - 1:c],
                                                          sums[:, c - 1, EG - 1:EG], ALU.add))
                    nc.vector.tensor_copy(totals[:], sums[:, :, EG - 1]).then_inc(totals_ready, 1)
                    dve.wait_ge(bases_ready, n + 1)
                    for c in range(chunks):
                        link(dve, nc.vector.tensor_scalar(first[:, c, :], first[:, c, :], spare[:, c:c + 1], None, ALU.add))

                @block.tensor
                def _(pe):
                    pe.wait_ge(totals_ready, n + 1)
                    nc.tensor.matmul(spare[:, 0:chunks], before[:], totals[:], start=True, stop=False)
                    nc.tensor.matmul(spare[:, 0:chunks], ones[:], lower[:], start=False, stop=True)\
                      .then_inc(bases_ready, 1)

        def rank_stream(part, lanes, n, chunks, bank):
            slots = len(lanes)
            dig, = tiles(part, f"rank{n}", slots, "dig")
            hot, = tiles(part, f"rank{n}", slots, "hot", shape=(chunks, GR))
            same, = tiles(part, f"rank{n}", slots, "same", dt=BF16)
            dig_col, inner = tiles(part, f"rank{n}", slots, "dig_col", "inner", shape=(J,))
            rank, = tiles(part, f"rank{n}", slots, "rank", shape=(J,), dt=I32)
            rec, = tiles(part, f"rank{n}", slots, "rec", shape=(J * 4,), dt=I32)
            LD = Steps(lanes, "loaded", ["digits", "columns", "records"], 16)
            DV = Steps(lanes, "dve_done", [f"hot{c}" for c in range(chunks)] + [f"inner{j}" for j in range(J)] + ["rank"])
            PE = Steps(lanes, "pe_done", ["lookup"])
            SC = Steps(lanes, "scattered", [f"record{j}" for j in range(J)], 16)

            def free(sp, k, b):
                wait_alone(sp, *SC.all(k, b))

            def sp_part(sp, step, k, b):
                if not is_first(k):
                    free(sp, k - 1, b)
                row = group_row(slots, k, b)
                load_digits(sp, n, dig[b], row, LD.sem[b])
                sp.dma_start(dig_col[b][:], dram_vec(digit[n], row)).then_inc(LD.sem[b], 16)
                sp.dma_start(rec[b][:], record[n][bass.ds(row, GR), :].rearrange("(p j) f -> p (j f)", j=J))\
                  .then_inc(LD.sem[b], 16)

            def dve_part(dve, step, k, b):
                if step.startswith("hot"):
                    c = int(step[-1])
                    dve.wait_ge(*LD.all(k, b))
                    nc.vector.tensor_scalar(hot[b][:, c, :], dig[b][:], iota_bin[:, c:c + 1], None, ALU.is_equal)\
                      .then_inc(DV.sem[b], 1)
                elif step.startswith("inner"):
                    j = int(step[-1])
                    if j:
                        dve.wait_ge(*DV.done(f"inner{j - 1}", k, b))
                    nc.vector.scalar_tensor_tensor(out=same[b][:], in0=dig[b][:], scalar=dig_col[b][:, j:j + 1],
                                                   in1=earlier[:, j, :], op0=ALU.is_equal, op1=ALU.mult,
                                                   accum_out=inner[b][:, j:j + 1]).then_inc(DV.sem[b], 1)
                elif step == "rank":
                    dve.wait_ge(*PE.done("lookup", k, b))
                    dve.wait_ge(*DV.done(f"inner{J - 1}", k, b))
                    nc.vector.tensor_tensor(rank[b][:], bank[:, 0:J], inner[b][:], ALU.add).then_inc(DV.sem[b], 1)

            def pe_part(pe, step, k, b):
                pe.wait_ge(*DV.done(f"hot{chunks - 1}", k, b))
                if b:
                    pe.wait_ge(*DV.done("rank", k, b - 1))
                elif not is_first(k):
                    pe.wait_ge(*DV.done("rank", k - 1, slots - 1))
                for j in range(J):
                    for c in range(chunks):
                        ins = nc.tensor.matmul(bank[:, j:j + 1], cols(hot[b][:, c, :], j),
                                               first[:, c, bass.ds(k * slots + b, 1)],
                                               start=(c == 0), stop=(c == chunks - 1))
                ins.then_inc(PE.sem[b], 1)

            def pool_part(pool, step, k, b):
                wait_alone(pool, *DV.done("rank", k, b))
                for j in range(J):
                    scatter(pool, record[n + 1], rank[b], rec[b][:, 4 * j:4 * j + 4], j, SC.sem[b])

            chain = [("sp", "load", 4)] + [("dve", f"hot{c}", 0.55) for c in range(chunks)]
            chain += [("dve", f"inner{j}", 0.81) for j in range(J)]
            chain += [("pe", "lookup", 3), ("dve", "rank", .5), ("pool", "scatter", 10)]
            return Stream(lanes, EG, chain, {"sp": sp_part, "dve": dve_part, "pe": pe_part, "pool": pool_part,
                                             "free": free}, (LD, DV, PE, SC))

        def chain_stream(part, lanes, banks, dense):
            slots = len(lanes)
            name = "dense" if dense else "chain"
            xr, xT, hT, z, xb, x1, x2 = tiles(part, name, slots, "xr", "xT", "hT", "z", "xb", "x1", "x2")
            stats, = tiles(part, name, slots, "stats", shape=(J, 6))
            moments, = tiles(part, name, slots, "moments", shape=(J, 2))
            root, root4, sums, inv_sq, keep, keep_sq, var4 = tiles(part, name, slots, "root", "root4", "sums", "inv_sq", "keep",
                                                                   "keep_sq", "var4", shape=(J,))
            idx, = tiles(part, name, slots, "idx", shape=(J,), dt=I32)
            if dense:
                h1 = h2 = None
                squares = xT
            else:
                h1, h2, sq = tiles(part, name, slots, "h1", "h2", "sq")
                squares = sq
            x3 = z if not dense else x1
            to_table = [] if dense else ["h1_rows"]
            to_table2 = [] if dense else ["h2_rows"]
            PE = Steps(lanes, "pe_done", ["xT", "upd_h", "upd_o", "x1T", "sage_h"] + to_table + ["sage_o", "x2T", "gcn_h"]
                       + to_table2 + ["gcn_o"] + (["sums"] if dense else []))
            AC = Steps(lanes, "act_done", ["xT", "upd_h", "ln0_root", "ln1_root", "x1T", "sage_h"] + to_table
                       + ["ln2_squares", "ln2_root", "x2T", "gcn_h"] + to_table2 + ["ln3_squares", "ln3_root"]
                       + (["ln4_root", "out"] if dense else []))
            DV = Steps(lanes, "dve_done", (["keep"] if dense else []) + ["z0", "ln0_stats", "ln0_moments", "ln0_inv",
                       "ln0_norm", "ln1_stats", "ln1_moments", "ln1_inv", "ln1_norm", "z2", "ln2_inv",
                       "ln2_norm", "z3", "ln3_inv"] + (["inv_sq", "var4"] if dense else []) + ["ln3_norm"]
                       + (["ln4_inv", "sums"] if dense else []))
            PO = Steps(lanes, "pool_done", ["xb", "ln0_w", "ln0_x"])
            GA = Steps(lanes, "gathered", [f"x{j}" for j in range(J)], 16)
            IX = Steps(lanes, "listed", ["idx"], 16)
            LD = Steps(lanes, "loaded", ["x"], 16)
            ST = Steps(lanes, "stored", ["out"] if dense else ["x1", "h1", "x2", "h2", "x3"], 16)
            rows_in = LD if dense else GA

            def last_group(k, b):
                return dense and isinstance(k, int) and k * slots + b == DG - 1

            def row_of(k, b):
                return N - GR if last_group(k, b) else group_row(slots, k, b)

            def free(sp, k, b):
                wait_alone(sp, *ST.all(k, b))
                wait_alone(sp, *DV.all(k, b))

            def sp_part(sp, step, k, b):
                row = row_of(k, b)
                if step == "load":
                    if not is_first(k):
                        free(sp, k - 1, b)
                    if dense:
                        sp.dma_start(xr[b][:], dram_rows(x, row)).then_inc(LD.sem[b], 16)
                        sp.dma_start(idx[b][:], slot_of[bass.ds(row, GR), :].rearrange("(p j) a -> p (j a)", j=J))\
                          .then_inc(IX.sem[b], 16)
                    else:
                        sp.dma_start(idx[b][:], dram_vec(src_gather_idx, row)).then_inc(IX.sem[b], 16)
                elif step == "out":
                    wait_alone(sp, *AC.done("out", k, b))
                    if last_group(k, b):
                        p0 = (DG * GR - N) // J
                        sp.dma_start(dram_rows(out, N - (P - p0) * J, (P - p0) * J), z[b][p0:P, :])\
                          .then_inc(ST.sem[b], 16)
                    else:
                        sp.dma_start(dram_rows(out, row), z[b][:]).then_inc(ST.sem[b], 16)
                else:
                    source, (ready, ready_step), table_n = {
                        "x1": (x1, (DV, "ln1_norm"), X1), "h1": (h1, (AC, "h1_rows"), H1),
                        "x2": (x2, (DV, "ln2_norm"), X2S), "h2": (h2, (AC, "h2_rows"), H2S),
                        "x3": (x3, (DV, "ln3_norm"), X3)}[step]
                    wait_alone(sp, *ready.done(ready_step, k, b))
                    sp.dma_start(dram_rows(table[table_n], row + EP), source[b][:]).then_inc(ST.sem[b], 16)

            def pool_part(pool, step, k, b):
                if step == "gather":
                    wait_alone(pool, *IX.all(k, b))
                    for j in range(J):
                        gather(pool, rows(xr[b], j), idx[b], x, j, GA.sem[b])
                elif step == "xb":
                    pool.wait_ge(*rows_in.all(k, b))
                    nc.gpsimd.tensor_tensor(xb[b][:], xr[b][:], ln_b[:], ALU.add).then_inc(PO.sem[b], 1)
                elif step == "ln0_w":
                    pool.wait_ge(*DV.done("ln0_norm", k, b))
                    nc.gpsimd.tensor_tensor(z[b][:], z[b][:], ln_w[:], ALU.mult).then_inc(PO.sem[b], 1)
                elif step == "ln0_x":
                    pool.wait_ge(*PO.done("ln0_w", k, b))
                    nc.gpsimd.tensor_tensor(z[b][:], z[b][:], xb[b][:], ALU.add).then_inc(PO.sem[b], 1)

            def pe_part(pe, step, k, b):
                bank = banks[b]
                if step == "xT":
                    pe.wait_ge(*rows_in.all(k, b))
                    ins = to_cols(bank, xr[b])
                elif step == "upd_h":
                    pe.wait_ge(*AC.done("xT", k, b))
                    ins = features(bank, (W["upd_x"], xT[b]))
                elif step == "upd_o":
                    pe.wait_ge(*AC.done("upd_h", k, b))
                    ins = nodes(bank, "upd_b2", (W["upd_out"], hT[b]))
                elif step == "x1T":
                    pe.wait_ge(*DV.done("ln1_norm", k, b))
                    ins = to_cols(bank, x1[b])
                elif step == "sage_h":
                    pe.wait_ge(*AC.done("x1T", k, b))
                    ins = features(bank, (W["sage1_r"], xT[b]))
                elif step == "h1_rows":
                    pe.wait_ge(*AC.done("sage_h", k, b))
                    ins = to_rows(bank, hT[b])
                elif step == "sage_o":
                    pe.wait_ge(*AC.done("sage_h" if dense else "h1_rows", k, b))
                    ins = nodes(bank, "sage_b2", (W["sage2_r"], hT[b]))
                elif step == "x2T":
                    pe.wait_ge(*DV.done("ln2_norm", k, b))
                    ins = to_cols(bank, x2[b])
                elif step == "gcn_h":
                    pe.wait_ge(*AC.done("x2T", k, b))
                    ins = features(bank, (W["gcn1"], xT[b]))
                elif step == "h2_rows":
                    pe.wait_ge(*AC.done("gcn_h", k, b))
                    ins = to_rows(bank, hT[b])
                elif step == "gcn_o":
                    pe.wait_ge(*AC.done("gcn_h" if dense else "h2_rows", k, b))
                    ins = nodes(bank, "gcn_b2", (W["gcn2"], hT[b]))
                elif step == "sums":
                    pe.wait_ge(*DV.done("ln3_norm", k, b))
                    ins = feature_sums(bank, x3[b], keep[b], squares[b], keep_sq[b])
                ins.then_inc(PE.sem[b], 1)

            def act_part(act, step, k, b):
                bank = banks[b]
                if step in ("xT", "x1T", "x2T"):
                    act.wait_ge(*PE.done(step, k, b))
                    ins = nc.scalar.activation(xT[b][:], bank[:], ACT.Copy)
                elif step in ("upd_h", "sage_h", "gcn_h"):
                    act.wait_ge(*PE.done(step, k, b))
                    bias = colb[{"upd_h": "upd_b1", "sage_h": "sage_b1", "gcn_h": "gcn_b1"}[step]]
                    ins = nc.scalar.activation(hT[b][:], bank[:], ACT.Relu, bias=bias[:])
                elif step in ("h1_rows", "h2_rows"):
                    act.wait_ge(*PE.done(step, k, b))
                    ins = nc.scalar.activation((h1 if step == "h1_rows" else h2)[b][:], bank[:], ACT.Copy)
                elif step in ("ln0_root", "ln1_root"):
                    act.wait_ge(*DV.done(step[:3] + "_moments", k, b))
                    ins = root_of(root[b], moments[b][:, :, 1])
                elif step in ("ln2_squares", "ln3_squares"):
                    act.wait_ge(*DV.done("z2" if step == "ln2_squares" else "z3", k, b))
                    ins = row_squares(squares[b], z[b], sums[b])
                elif step in ("ln2_root", "ln3_root"):
                    act.wait_ge(*AC.done(step[:3] + "_squares", k, b))
                    ins = root_of_sums(root[b], sums[b])
                elif step == "ln4_root":
                    act.wait_ge(*DV.done("var4", k, b))
                    ins = root_of_sums(root4[b], var4[b])
                elif step == "out":
                    act.wait_ge(*DV.done("ln4_inv", k, b))
                    ins = act_scale_rows(z[b], x3[b], root4[b])
                ins.then_inc(AC.sem[b], 1)

            def dve_part(dve, step, k, b):
                if step == "keep":
                    dve.wait_ge(*IX.all(k, b))
                    if last_group(k, b):
                        ins = nc.vector.tensor_scalar(keep[b][:], idx[b][:], 0.0, last_group_keep[:], ALU.is_lt, ALU.mult)
                    else:
                        ins = nc.vector.tensor_scalar(keep[b][:], idx[b][:], 0.0, None, ALU.is_lt)
                elif step in ("z0", "z2", "z3"):
                    made, residual = {"z0": ("upd_o", xr), "z2": ("sage_o", x1), "z3": ("gcn_o", x2)}[step]
                    dve.wait_ge(*PE.done(made, k, b))
                    ins = nc.vector.tensor_tensor(z[b][:], banks[b][:], residual[b][:], ALU.add)
                elif step in ("ln0_stats", "ln1_stats"):
                    dve.wait_ge(*(DV.done("z0", k, b) if step == "ln0_stats" else PO.done("ln0_x", k, b)))
                    ins = row_stats(stats[b], z[b])
                elif step in ("ln0_moments", "ln1_moments"):
                    wait_alone(dve, *DV.done(step[:3] + "_stats", k, b))
                    ins = row_moments(moments[b], stats[b])
                elif step in ("ln0_inv", "ln1_inv", "ln2_inv", "ln3_inv", "ln4_inv"):
                    dve.wait_ge(*AC.done(step[:3] + "_root", k, b))
                    inv = (root4 if step == "ln4_inv" else root)[b]
                    ins = nc.vector.reciprocal(inv[:], inv[:])
                elif step in ("ln0_norm", "ln1_norm"):
                    dve.wait_ge(*DV.done(step[:3] + "_inv", k, b))
                    ins = norm_rows((z if step == "ln0_norm" else x1)[b], z[b], moments[b], root[b])
                elif step == "ln2_norm":
                    dve.wait_ge(*DV.done("ln2_inv", k, b))
                    ins = scale_rows(x2[b], z[b], root[b])
                elif step == "inv_sq":
                    dve.wait_ge(*DV.done("ln3_inv", k, b))
                    ins = nc.vector.tensor_tensor(inv_sq[b][:], root[b][:], root[b][:], ALU.mult)
                elif step == "var4":
                    dve.wait_ge(*DV.done("inv_sq", k, b))
                    nc.vector.tensor_tensor(keep_sq[b][:], inv_sq[b][:], keep[b][:], ALU.mult)
                    ins = nc.vector.tensor_tensor(var4[b][:], inv_sq[b][:], sums[b][:], ALU.mult)
                elif step == "ln3_norm":
                    dve.wait_ge(*DV.done("ln3_inv", k, b))
                    ins = scale_rows(x3[b], z[b], root[b])
                elif step == "sums":
                    dve.wait_ge(*PE.done("sums", k, b))
                    ins = nc.vector.tensor_tensor(bn_part[b][:], bn_part[b][:], banks[b][:, 0:2], ALU.add)
                ins.then_inc(DV.sem[b], 1)

            chain = [("sp", "load", 2.55)]
            chain += [("dve", "keep", 0.1)] if dense else [("pool", "gather", 7)]
            chain += [("pool", "xb", 0.12), ("pe", "xT", 0.5), ("act", "xT", 0.5), ("pe", "upd_h", 1.2), ("act", "upd_h", 1.2),
                      ("pe", "upd_o", 1.47), ("dve", "z0", 0.85), ("dve", "ln0_stats", 0.65), ("dve", "ln0_moments", 0.7),
                      ("act", "ln0_root", 0.5), ("dve", "ln0_inv", 0.21), ("dve", "ln0_norm", 1.72), ("pool", "ln0_w", 1.68),
                      ("pool", "ln0_x", 2.02), ("dve", "ln1_stats", 1.3), ("dve", "ln1_moments", 0.9), ("act", "ln1_root", 0.35),
                      ("dve", "ln1_inv", 0.3), ("dve", "ln1_norm", 1.22)]
            chain += [] if dense else [("sp", "x1", 0)]
            chain += [("pe", "x1T", 0.9), ("act", "x1T", 0.9), ("pe", "sage_h", 1.2), ("act", "sage_h", 1.2)]
            chain += [] if dense else [("pe", "h1_rows", .5), ("act", "h1_rows", .7), ("sp", "h1", 0)]
            chain += [("pe", "sage_o", 2.1), ("dve", "z2", 0.85), ("act", "ln2_squares", 2.7), ("act", "ln2_root", 0.4),
                      ("dve", "ln2_inv", 0.42), ("dve", "ln2_norm", 0.34)]
            chain += [] if dense else [("sp", "x2", 0)]
            chain += [("pe", "x2T", 0.5), ("act", "x2T", 0.5), ("pe", "gcn_h", 0.61), ("act", "gcn_h", 0.61)]
            chain += [] if dense else [("pe", "h2_rows", .5), ("act", "h2_rows", .7), ("sp", "h2", 0)]
            chain += [("pe", "gcn_o", 2.1), ("dve", "z3", 1.68), ("act", "ln3_squares", 1.05), ("act", "ln3_root", 0.72),
                      ("dve", "ln3_inv", 0.36)]
            chain += [("dve", "inv_sq", 0.2), ("dve", "var4", 0.3), ("act", "ln4_root", 0.0)] if dense else []
            chain += [("dve", "ln3_norm", 1.44)]
            chain += [("dve", "ln4_inv", 0.17), ("pe", "sums", 0.5), ("act", "out", 1.65), ("dve", "sums", 0.5), ("sp", "out", 1.65)]\
                if dense else [("sp", "x3", 3)]
            return Stream(lanes, DG if dense else EG, chain, {"sp": sp_part, "pool": pool_part, "pe": pe_part, "act": act_part,
                                             "dve": dve_part, "free": free},
                          (PE, AC, DV, PO, ST, IX, rows_in))

        def message_stream(part, lanes, banks):
            slots = len(lanes)
            sr, tr, er, sT, tT, eT, agg, xb, mask = tiles(part, "msg", slots, "sr", "tr", "er", "sT", "tT", "eT", "agg",
                                                          "xb", "mask")
            s_idx, t_idx = tiles(part, "msg", slots, "s_idx", "t_idx", shape=(J,), dt=I32)
            stats, = tiles(part, "msg", slots, "stats", shape=(J, 6))
            moments, = tiles(part, "msg", slots, "moments", shape=(J, 2))
            root, = tiles(part, "msg", slots, "root", shape=(J,))
            z, x1 = sr, er
            PE = Steps(lanes, "pe_done", ["sT", "tT", "eT", "msg_h", "msg", "upd_h", "upd_o"])
            AC = Steps(lanes, "act_done", ["sT", "tT", "eT", "msg_h", "msg", "upd_h", "ln0_root", "ln1_root"])
            DV = Steps(lanes, "dve_done", ["agg", "z0", "ln0_stats", "ln0_moments", "ln0_inv", "ln0_norm", "ln0_w", "ln0_x",
                                           "ln1_stats", "ln1_moments", "ln1_inv", "ln1_norm"])
            PO = Steps(lanes, "pool_done", ["xb"])
            LD = Steps(lanes, "loaded", ["edge", "mask"], 16)
            IX = Steps(lanes, "listed", ["s", "t"], 16)
            GA = Steps(lanes, "gathered", [f"{n}{j}" for n in "st" for j in range(J)], 16)
            ST = Steps(lanes, "stored", ["x1"], 16)
            start_sums((agg,))

            def free(sp, k, b):
                wait_alone(sp, *ST.all(k, b))

            def sp_part(sp, step, k, b):
                row = group_row(slots, k, b)
                if step == "load":
                    if not is_first(k):
                        free(sp, k - 1, b)
                    sp.dma_start(s_idx[b][:], dram_vec(src_gather_idx, row)).then_inc(IX.sem[b], 16)
                    sp.dma_start(t_idx[b][:], dram_vec(dst_gather_idx, row)).then_inc(IX.sem[b], 16)
                    if isinstance(row, int) and row + GR > E:
                        left = E - row
                        sp.dma_start(er[b][0:left // J, :], dram_rows(edge_attr, row, left)).then_inc(LD.sem[b], 16)
                    else:
                        sp.dma_start(er[b][:], dram_rows(edge_attr, row)).then_inc(LD.sem[b], 16)
                    sp.dma_start(mask[b][:], edge_rows[bass.ds(k * slots + b, 1), MASK, :]
                                 .rearrange("a c -> (a c)").partition_broadcast(P)).then_inc(LD.sem[b], 16)
                elif step == "store":
                    wait_alone(sp, *DV.done("ln1_norm", k, b))
                    sp.dma_start(dram_rows(table[X1], row), x1[b][:]).then_inc(ST.sem[b], 16)

            def pool_part(pool, step, k, b):
                if step == "gather":
                    wait_alone(pool, *IX.all(k, b))
                    for j in range(J):
                        gather(pool, rows(sr[b], j), s_idx[b], x, j, GA.sem[b])
                    for j in range(J):
                        gather(pool, rows(tr[b], j), t_idx[b], x, j, GA.sem[b])
                elif step == "xb":
                    pool.wait_ge(*GA.all(k, b))
                    nc.gpsimd.tensor_tensor(xb[b][:], tr[b][:], ln_b[:], ALU.add).then_inc(PO.sem[b], 1)

            def pe_part(pe, step, k, b):
                bank = banks[b]
                if step == "sT":
                    pe.wait_ge(*GA.all(k, b))
                    ins = to_cols(bank, sr[b])
                elif step == "tT":
                    pe.wait_ge(*AC.done("sT", k, b))
                    ins = to_cols(bank, tr[b])
                elif step == "eT":
                    pe.wait_ge(*LD.all(k, b))
                    pe.wait_ge(*AC.done("tT", k, b))
                    ins = to_cols(bank, er[b])
                elif step == "msg_h":
                    pe.wait_ge(*AC.done("eT", k, b))
                    ins = features(bank, (W["msg_src"], sT[b]), (W["msg_dst"], tT[b]), (W["msg_edge"], eT[b]))
                elif step == "msg":
                    pe.wait_ge(*AC.done("msg_h", k, b))
                    ins = features(bank, (W["msg_out"], sT[b]))
                elif step == "upd_h":
                    pe.wait_ge(*DV.done("agg", k, b))
                    ins = features(bank, (W["upd_x"], tT[b]), (W["upd_agg"], agg[b]))
                elif step == "upd_o":
                    pe.wait_ge(*AC.done("upd_h", k, b))
                    ins = nodes(bank, "upd_b2", (W["upd_out"], sT[b]))
                ins.then_inc(PE.sem[b], 1)

            def act_part(act, step, k, b):
                if step in ("ln0_root", "ln1_root"):
                    act.wait_ge(*DV.done(step[:3] + "_moments", k, b))
                    root_of(root[b], moments[b][:, :, 1]).then_inc(AC.sem[b], 1)
                    return
                act.wait_ge(*PE.done(step, k, b))
                target, func, bias = {
                    "sT": (sT, ACT.Copy, None), "tT": (tT, ACT.Copy, None), "eT": (eT, ACT.Copy, None),
                    "msg_h": (sT, ACT.Relu, "msg_b1"), "msg": (eT, ACT.Identity, "msg_b2"),
                    "upd_h": (sT, ACT.Relu, "upd_b1")}[step]
                more = {"bias": colb[bias][:]} if bias else {}
                nc.scalar.activation(target[b][:], banks[b][:], func, **more).then_inc(AC.sem[b], 1)

            def dve_part(dve, step, k, b):
                if step == "agg":
                    dve.wait_ge(*LD.all(k, b))
                    dve.wait_ge(*AC.done("msg", k, b))
                    carried(dve, DV, "agg", k, b, slots)
                    ins = nc.vector.tensor_tensor_scan(agg[b][:], mask[b][:], eT[b][:], agg[b - 1][:, GR - 1:GR],
                                                       ALU.mult, ALU.add)
                elif step == "z0":
                    dve.wait_ge(*PE.done("upd_o", k, b))
                    ins = nc.vector.tensor_tensor(z[b][:], banks[b][:], tr[b][:], ALU.add)
                elif step in ("ln0_stats", "ln1_stats"):
                    dve.wait_ge(*DV.done("z0" if step == "ln0_stats" else "ln0_x", k, b))
                    ins = row_stats(stats[b], z[b])
                elif step in ("ln0_moments", "ln1_moments"):
                    wait_alone(dve, *DV.done(step[:3] + "_stats", k, b))
                    ins = row_moments(moments[b], stats[b])
                elif step in ("ln0_inv", "ln1_inv"):
                    dve.wait_ge(*AC.done(step[:3] + "_root", k, b))
                    ins = nc.vector.reciprocal(root[b][:], root[b][:])
                elif step in ("ln0_norm", "ln1_norm"):
                    dve.wait_ge(*DV.done(step[:3] + "_inv", k, b))
                    ins = norm_rows((z if step == "ln0_norm" else x1)[b], z[b], moments[b], root[b])
                elif step == "ln0_w":
                    dve.wait_ge(*DV.done("ln0_norm", k, b))
                    ins = nc.vector.tensor_tensor(z[b][:], z[b][:], ln_w[:], ALU.mult)
                elif step == "ln0_x":
                    dve.wait_ge(*DV.done("ln0_w", k, b))
                    dve.wait_ge(*PO.done("xb", k, b))
                    ins = nc.vector.tensor_tensor(z[b][:], z[b][:], xb[b][:], ALU.add)
                ins.then_inc(DV.sem[b], 1)

            chain = [("sp", "load", 3), ("pool", "gather", 11), ("pool", "xb", .2), ("pe", "sT", .5), ("act", "sT", .7),
                     ("pe", "tT", .5), ("act", "tT", .7), ("pe", "eT", .5), ("act", "eT", .7), ("pe", "msg_h", 3),
                     ("act", "msg_h", .7), ("pe", "msg", 1.2), ("act", "msg", .7), ("dve", "agg", 1.6),
                     ("pe", "upd_h", 2), ("act", "upd_h", .7), ("pe", "upd_o", 1.5), ("dve", "z0", 1),
                     ("dve", "ln0_stats", 1), ("dve", "ln0_moments", .5),
                     ("act", "ln0_root", .5), ("dve", "ln0_inv", .3), ("dve", "ln0_norm", .8), ("dve", "ln0_w", .8),
                     ("dve", "ln0_x", .8), ("dve", "ln1_stats", 1), ("dve", "ln1_moments", .5), ("act", "ln1_root", .5),
                     ("dve", "ln1_inv", .3), ("dve", "ln1_norm", .8), ("sp", "store", 3)]
            return Stream(lanes, EG, chain, {"sp": sp_part, "pool": pool_part, "pe": pe_part, "act": act_part,
                                             "dve": dve_part, "free": free}, (PE, AC, DV, PO, LD, IX, GA, ST))

        def edge_stream(part, lanes, banks, stage):
            slots = len(lanes)
            name = f"edge{stage}"
            gcn = stage >= 3
            hidden = stage in (1, 3)
            sr, tr, agg, v = tiles(part, name, slots, "sr", "tr", "agg", "v")
            tT = tiles(part, name, slots, "tT")[0] if stage != 3 else None
            yT, y = (sr, tr) if hidden else (None, v)
            mask, scale = tiles(part, name, slots, "mask", "scale")
            weight = tiles(part, name, slots, "weight")[0] if gcn else None
            res = tiles(part, name, slots, "res")[0] if not hidden else None
            dis_col, end_col, root, root4, sums, inv_sq, end_sq, var4 = tiles(
                part, name, slots, "dis_col", "end_col", "root", "root4", "sums", "inv_sq", "end_sq", "var4", shape=(J,))
            s_idx, o_idx = tiles(part, name, slots, "s_idx", "o_idx", shape=(J,), dt=I32)
            source = {1: X1, 2: H1, 3: X2S, 4: H2S}[stage]
            z, squares = tr, tT
            PE = Steps(lanes, "pe_done", ["sT", "tT"] + {
                1: ["h", "rows"], 2: ["o"], 3: ["h", "rows"], 4: ["o", "sums"]}[stage])
            AC = Steps(lanes, "act_done", {1: ["tT", "h", "rows"], 2: ["tT", "squares", "root", "by_dis"], 3: ["h", "rows"],
                                           4: ["squares", "root", "ln4_root", "out"]}[stage])
            DV = Steps(lanes, "dve_done", {
                1: ["agg", "mean"],
                2: ["agg", "mean", "z", "inv", "norm"],
                3: ["weighted", "agg", "self", "scaled", "h_scaled"],
                4: ["weighted", "agg", "self", "scaled", "z", "inv", "inv_sq", "var4", "norm", "ln4_inv", "sums"]}[stage])
            LD = Steps(lanes, "loaded", ["t", "mask", "scale"] + (["weight"] if gcn else []) + (["res"] if not hidden else [])
                       + {2: ["dis_col"], 4: ["end_col"]}.get(stage, []), 16)
            IX = Steps(lanes, "listed", ["s"] + (["o"] if stage == 4 else []), 16)
            GA = Steps(lanes, "gathered", [f"s{j}" for j in range(J)], 16)
            ST = Steps(lanes, "stored", {1: ["h1"], 2: ["x2", "x2s"], 3: ["h2s"], 4: ["x3"]}[stage], 16)
            SC = Steps(lanes, "scattered", [f"out{j}" for j in range(J)], 16) if stage == 4 else None
            start_sums((agg,))

            def free(sp, k, b):
                wait_alone(sp, *ST.all(k, b))
                if stage == 4:
                    wait_alone(sp, *SC.all(k, b))
                    wait_alone(sp, *DV.all(k, b))

            def sp_part(sp, step, k, b):
                row = group_row(slots, k, b)

                def row_of_group(r):
                    return edge_rows[bass.ds(k * slots + b, 1), r, :].rearrange("a c -> (a c)").partition_broadcast(P)

                if step == "load":
                    if not is_first(k):
                        free(sp, k - 1, b)
                    sp.dma_start(s_idx[b][:], dram_vec(src_row, row)).then_inc(IX.sem[b], 16)
                    if stage == 4:
                        sp.dma_start(o_idx[b][:], dram_vec(dst_out_idx, row)).then_inc(IX.sem[b], 16)
                    sp.dma_start(tr[b][:], dram_rows(table[source], row)).then_inc(LD.sem[b], 16)
                    sp.dma_start(mask[b][:], row_of_group(MASK)).then_inc(LD.sem[b], 16)
                    sp.dma_start(scale[b][:], row_of_group(DIS if gcn else INV)).then_inc(LD.sem[b], 16)
                    if gcn:
                        sp.dma_start(weight[b][:], row_of_group(EW)).then_inc(LD.sem[b], 16)
                    if not hidden:
                        sp.dma_start(res[b][:], dram_rows(table[X1] if stage == 2 else x2_plain, row))\
                          .then_inc(LD.sem[b], 16)
                    if stage == 2:
                        sp.dma_start(dis_col[b][:], edge_rows[bass.ds(k * slots + b, 1), DIS, :]
                                     .rearrange("a (p j) -> p (a j)", j=J)).then_inc(LD.sem[b], 16)
                    if stage == 4:
                        sp.dma_start(end_col[b][:], dram_vec(is_end, row)).then_inc(LD.sem[b], 16)
                elif step == "store":
                    if hidden:
                        wait_alone(sp, *AC.done("rows", k, b))
                        sp.dma_start(dram_rows(table[H1 if stage == 1 else H2S], row), y[b][:]).then_inc(ST.sem[b], 16)
                    elif stage == 2:
                        wait_alone(sp, *AC.done("by_dis", k, b))
                        sp.dma_start(dram_rows(x2_plain, row), y[b][:]).then_inc(ST.sem[b], 16)
                        sp.dma_start(dram_rows(table[X2S], row), sr[b][:]).then_inc(ST.sem[b], 16)
                    else:
                        wait_alone(sp, *DV.done("norm", k, b))
                        sp.dma_start(dram_rows(table[X3], row), y[b][:]).then_inc(ST.sem[b], 16)

            def pool_part(pool, step, k, b):
                if step == "gather":
                    wait_alone(pool, *IX.all(k, b))
                    for j in range(J):
                        gather(pool, rows(sr[b], j), s_idx[b], table[source], j, GA.sem[b])
                elif step == "scatter":
                    wait_alone(pool, *AC.done("out", k, b))
                    for j in range(J):
                        scatter(pool, out, o_idx[b], rows(sr[b], j), j, SC.sem[b], limit=N - 1)

            def pe_part(pe, step, k, b):
                bank = banks[b]
                if step == "sT":
                    pe.wait_ge(*GA.all(k, b))
                    ins = to_cols(bank, sr[b])
                elif step == "tT":
                    pe.wait_ge(*LD.all(k, b))
                    pe.wait_ge(*DV.done("weighted" if gcn else "agg", k, b))
                    ins = to_cols(bank, tr[b])
                elif step in ("h", "o"):
                    pe.wait_ge(*DV.done("scaled" if gcn else "mean", k, b))
                    if not gcn:
                        pe.wait_ge(*AC.done("tT", k, b))
                    if stage == 1:
                        ins = features(bank, (W["sage1_l"], v[b]), (W["sage1_r"], tT[b]))
                    elif stage == 2:
                        ins = nodes(bank, "sage_b2", (W["sage2_l"], v[b]), (W["sage2_r"], tT[b]))
                    elif stage == 3:
                        ins = features(bank, (W["gcn1"], v[b]))
                    else:
                        ins = nodes(bank, "gcn_b2", (W["gcn2"], v[b]))
                elif step == "rows":
                    if gcn:
                        pe.wait_ge(*DV.done("h_scaled", k, b))
                    else:
                        pe.wait_ge(*AC.done("h", k, b))
                    ins = to_rows(bank, yT[b])
                elif step == "sums":
                    pe.wait_ge(*DV.done("norm", k, b))
                    ins = feature_sums(bank, y[b], end_col[b], squares[b], end_sq[b])
                ins.then_inc(PE.sem[b], 1)

            def act_part(act, step, k, b):
                if step in ("tT", "h", "rows"):
                    act.wait_ge(*PE.done(step, k, b))
                    if step == "tT":
                        ins = nc.scalar.activation(tT[b][:], banks[b][:], ACT.Copy)
                    elif step == "h":
                        ins = nc.scalar.activation(yT[b][:], banks[b][:], ACT.Relu,
                                                   bias=colb["gcn_b1" if gcn else "sage_b1"][:])
                    else:
                        ins = nc.scalar.activation(y[b][:], banks[b][:], ACT.Copy)
                elif step == "squares":
                    act.wait_ge(*DV.done("z", k, b))
                    ins = row_squares(squares[b], z[b], sums[b])
                elif step == "root":
                    act.wait_ge(*AC.done("squares", k, b))
                    ins = root_of_sums(root[b], sums[b])
                elif step == "by_dis":
                    act.wait_ge(*DV.done("norm", k, b))
                    ins = act_scale_rows(sr[b], y[b], dis_col[b])
                elif step == "ln4_root":
                    act.wait_ge(*DV.done("var4", k, b))
                    ins = root_of_sums(root4[b], var4[b])
                elif step == "out":
                    act.wait_ge(*DV.done("ln4_inv", k, b))
                    ins = act_scale_rows(sr[b], y[b], root4[b])
                ins.then_inc(AC.sem[b], 1)

            def dve_part(dve, step, k, b):
                if step == "weighted":
                    dve.wait_ge(*LD.all(k, b))
                    dve.wait_ge(*PE.done("sT", k, b))
                    ins = nc.vector.tensor_tensor(v[b][:], banks[b][:], weight[b][:], ALU.mult)
                elif step == "agg":
                    if gcn:
                        dve.wait_ge(*DV.done("weighted", k, b))
                    else:
                        dve.wait_ge(*LD.all(k, b))
                        dve.wait_ge(*PE.done("sT", k, b))
                    carried(dve, DV, "agg", k, b, slots)
                    ins = nc.vector.tensor_tensor_scan(agg[b][:], mask[b][:], (v[b] if gcn else banks[b])[:],
                                                       agg[b - 1][:, GR - 1:GR], ALU.mult, ALU.add)
                elif step == "self":
                    dve.wait_ge(*DV.done("agg", k, b))
                    dve.wait_ge(*PE.done("tT", k, b))
                    ins = nc.vector.tensor_tensor(v[b][:], banks[b][:], agg[b][:], ALU.add)
                elif step == "scaled":
                    dve.wait_ge(*DV.done("self", k, b))
                    ins = nc.vector.tensor_tensor(v[b][:], v[b][:], scale[b][:], ALU.mult)
                elif step == "mean":
                    dve.wait_ge(*DV.done("agg", k, b))
                    ins = nc.vector.tensor_tensor(v[b][:], agg[b][:], scale[b][:], ALU.mult)
                elif step == "h_scaled":
                    dve.wait_ge(*AC.done("h", k, b))
                    ins = nc.vector.tensor_tensor(yT[b][:], yT[b][:], scale[b][:], ALU.mult)
                elif step == "z":
                    dve.wait_ge(*PE.done("o", k, b))
                    ins = nc.vector.tensor_tensor(z[b][:], banks[b][:], res[b][:], ALU.add)
                elif step in ("inv", "ln4_inv"):
                    dve.wait_ge(*AC.done("root" if step == "inv" else "ln4_root", k, b))
                    inv = (root if step == "inv" else root4)[b]
                    ins = nc.vector.reciprocal(inv[:], inv[:])
                elif step == "inv_sq":
                    dve.wait_ge(*DV.done("inv", k, b))
                    ins = nc.vector.tensor_tensor(inv_sq[b][:], root[b][:], root[b][:], ALU.mult)
                elif step == "var4":
                    dve.wait_ge(*DV.done("inv_sq", k, b))
                    nc.vector.tensor_tensor(end_sq[b][:], inv_sq[b][:], end_col[b][:], ALU.mult)
                    ins = nc.vector.tensor_tensor(var4[b][:], inv_sq[b][:], sums[b][:], ALU.mult)
                elif step == "norm":
                    dve.wait_ge(*DV.done("inv", k, b))
                    ins = scale_rows(y[b], z[b], root[b])
                elif step == "sums":
                    dve.wait_ge(*PE.done("sums", k, b))
                    ins = nc.vector.tensor_tensor(bn_part[b][:], bn_part[b][:], banks[b][:, 0:2], ALU.add)
                ins.then_inc(DV.sem[b], 1)

            chain = [("sp", "load", 3 if stage == 2 else 5), ("pool", "gather", 8), ("pe", "sT", .5)]
            chain += [("dve", "weighted", .9)] if gcn else []
            chain += [("dve", "agg", 1.5), ("pe", "tT", .5)]
            chain += [("dve", "self", .9), ("dve", "scaled", .8)] if gcn else [("act", "tT", .5), ("dve", "mean", .8)]
            if hidden:
                chain += [("pe", "h", 2), ("act", "h", .7)]
                chain += [("dve", "h_scaled", .8)] if gcn else []
                chain += [("pe", "rows", .5), ("act", "rows", .7), ("sp", "store", 3)]
            else:
                chain += [("pe", "o", 2), ("dve", "z", 1), ("act", "squares", 1.3), ("act", "root", .4), ("dve", "inv", .3)]
                chain += [("dve", "inv_sq", .2), ("dve", "var4", .3)] if stage == 4 else []
                chain += [("dve", "norm", .8)]
                chain += [("act", "by_dis", 1), ("sp", "store", 3)] if stage == 2 else [
                    ("sp", "store", 0), ("act", "ln4_root", .4), ("dve", "ln4_inv", .3), ("pe", "sums", .6), ("act", "out", 1),
                    ("dve", "sums", .2), ("pool", "scatter", 7)]
            return Stream(lanes, EG, chain, {"sp": sp_part, "pool": pool_part, "pe": pe_part, "act": act_part,
                                             "dve": dve_part, "free": free},
                          (PE, AC, DV, LD, IX, GA, ST) + ((SC,) if SC else ()))

        def attention_stream(part, lanes, banks):
            slots = len(lanes)
            sr, dr, mask, xns, xnd, t1, t2, num, den = tiles(part, "att", slots, "sr", "dr", "mask", "xns", "xnd", "t1", "t2",
                                                             "num", "den")
            s_idx, d_idx, o_idx = tiles(part, "att", slots, "s_idx", "d_idx", "o_idx", shape=(J,), dt=I32)
            stats, = tiles(part, "att", slots, "stats", shape=(J, 6))
            moments, = tiles(part, "att", slots, "moments", shape=(J, 2))
            root, inv_den = tiles(part, "att", slots, "root", "inv_den", shape=(J,))
            PE = Steps(lanes, "pe_done", ["sT", "k1", "sum1", "dT", "k2", "sum2", "den_rows", "map"])
            AC = Steps(lanes, "act_done", ["sT", "tanh1", "dT", "tanh2", "exp", "relu", "root"])
            DV = Steps(lanes, "dve_done", ["quad1", "quad2", "score", "leaky", "weighted", "num", "den", "inv_den", "z",
                                           "stats", "moments", "inv", "norm"])
            LD = Steps(lanes, "loaded", ["mask"], 16)
            IX = Steps(lanes, "listed", ["s", "d", "o"], 16)
            GA = Steps(lanes, "gathered", [f"{n}{j}" for n in "sd" for j in range(J)], 16)
            SC = Steps(lanes, "scattered", [f"out{j}" for j in range(J)], 16)
            start_sums((num, den))

            def free(sp, k, b):
                wait_alone(sp, *SC.all(k, b))

            def sp_part(sp, step, k, b):
                if not is_first(k):
                    free(sp, k - 1, b)
                row = group_row(slots, k, b)
                for t, v in ((s_idx, sorted_src_row), (d_idx, sorted_dst_row), (o_idx, src_out_idx)):
                    sp.dma_start(t[b][:], dram_vec(v, row)).then_inc(IX.sem[b], 16)
                sp.dma_start(mask[b][:], sorted_mask[bass.ds(row, GR)].partition_broadcast(P)).then_inc(LD.sem[b], 16)

            def pool_part(pool, step, k, b):
                if step == "gather":
                    wait_alone(pool, *IX.all(k, b))
                    for t, idx in ((sr, s_idx), (dr, d_idx)):
                        for j in range(J):
                            gather(pool, rows(t[b], j), idx[b], table[X3], j, GA.sem[b])
                elif step == "scatter":
                    wait_alone(pool, *DV.done("norm", k, b))
                    for j in range(J):
                        scatter(pool, out, o_idx[b], rows(t2[b], j), j, SC.sem[b], limit=N - 1)

            def pe_part(pe, step, k, b):
                bank = banks[b]
                if step == "sT":
                    pe.wait_ge(*GA.all(k, b))
                    ins = to_cols(bank, sr[b])
                elif step == "k1":
                    pe.wait_ge(*AC.done("sT", k, b))
                    ins = features(bank, (W["k1"], xns[b]))
                elif step == "sum1":
                    pe.wait_ge(*DV.done("quad1", k, b))
                    ins = features(bank, (ones, t1[b]))
                elif step == "dT":
                    pe.wait_ge(*AC.done("tanh1", k, b))
                    ins = to_cols(bank, dr[b])
                elif step == "k2":
                    pe.wait_ge(*AC.done("dT", k, b))
                    ins = features(bank, (W["k2"], xnd[b]))
                elif step == "sum2":
                    pe.wait_ge(*DV.done("quad2", k, b))
                    ins = features(bank, (ones, t2[b]))
                elif step == "den_rows":
                    pe.wait_ge(*DV.done("den", k, b))
                    for j in range(J):
                        ins = nc.tensor.matmul(bank[:, j:j + 1], cols(den[b][0:1, :], j), ones[0:1, 0:1],
                                               start=True, stop=True)
                elif step == "map":
                    pe.wait_ge(*DV.done("inv_den", k, b))
                    ins = nodes(bank, None, (W["map"], num[b]))
                ins.then_inc(PE.sem[b], 1)

            def act_part(act, step, k, b):
                if step in ("sT", "dT"):
                    act.wait_ge(*PE.done(step, k, b))
                    ins = nc.scalar.activation((xns if step == "sT" else xnd)[b][:], banks[b][:], ACT.Identity,
                                               scale=bn_a[:], bias=bn_c[:])
                elif step in ("tanh1", "tanh2"):
                    act.wait_ge(*PE.done("sum1" if step == "tanh1" else "sum2", k, b))
                    ins = nc.scalar.activation((t1 if step == "tanh1" else t2)[b][:], banks[b][:], ACT.Tanh)
                elif step == "exp":
                    act.wait_ge(*DV.done("leaky", k, b))
                    ins = nc.scalar.activation(t1[b][:], t2[b][:], ACT.Exp)
                elif step == "relu":
                    act.wait_ge(*PE.done("map", k, b))
                    for j in range(J):
                        ins = nc.scalar.activation(rows(dr[b], j), rows(banks[b], j), ACT.Relu, scale=inv_den[b][:, j:j + 1])
                elif step == "root":
                    act.wait_ge(*DV.done("moments", k, b))
                    ins = root_of(root[b], moments[b][:, :, 1])
                ins.then_inc(AC.sem[b], 1)

            def dve_part(dve, step, k, b):
                if step == "quad1":
                    dve.wait_ge(*PE.done("k1", k, b))
                    ins = nc.vector.tensor_tensor(t1[b][:], banks[b][:], xns[b][:], ALU.mult)
                elif step == "quad2":
                    dve.wait_ge(*PE.done("k2", k, b))
                    ins = nc.vector.tensor_tensor(t2[b][:], banks[b][:], xnd[b][:], ALU.mult)
                elif step == "score":
                    dve.wait_ge(*AC.done("tanh2", k, b))
                    ins = nc.vector.tensor_tensor(t1[b][:], t1[b][:], t2[b][:], ALU.add)
                elif step == "leaky":
                    dve.wait_ge(*DV.done("score", k, b))
                    ins = nc.vector.scalar_tensor_tensor(out=t2[b][:], in0=t1[b][:], scalar=0.01, in1=t1[b][:],
                                                         op0=ALU.mult, op1=ALU.max)
                elif step == "weighted":
                    dve.wait_ge(*AC.done("exp", k, b))
                    ins = nc.vector.tensor_tensor(xns[b][:], t1[b][:], xnd[b][:], ALU.mult)
                elif step == "num":
                    dve.wait_ge(*LD.all(k, b))
                    dve.wait_ge(*DV.done("weighted", k, b))
                    carried(dve, DV, "num", k, b, slots)
                    ins = nc.vector.tensor_tensor_scan(num[b][:], mask[b][:], xns[b][:], num[b - 1][:, GR - 1:GR],
                                                       ALU.mult, ALU.add)
                elif step == "den":
                    carried(dve, DV, "den", k, b, slots)
                    ins = nc.vector.tensor_tensor_scan(den[b][:], mask[b][:], t1[b][:], den[b - 1][:, GR - 1:GR],
                                                       ALU.mult, ALU.add)
                elif step == "inv_den":
                    dve.wait_ge(*PE.done("den_rows", k, b))
                    ins = nc.vector.reciprocal(inv_den[b][:], banks[b][:, 0:J])
                elif step == "z":
                    dve.wait_ge(*AC.done("relu", k, b))
                    ins = nc.vector.tensor_tensor(dr[b][:], dr[b][:], sr[b][:], ALU.add)
                elif step == "stats":
                    dve.wait_ge(*DV.done("z", k, b))
                    ins = row_stats(stats[b], dr[b])
                elif step == "moments":
                    wait_alone(dve, *DV.done("stats", k, b))
                    ins = row_moments(moments[b], stats[b])
                elif step == "inv":
                    dve.wait_ge(*AC.done("root", k, b))
                    ins = nc.vector.reciprocal(root[b][:], root[b][:])
                elif step == "norm":
                    dve.wait_ge(*DV.done("inv", k, b))
                    ins = norm_rows(t2[b], dr[b], moments[b], root[b])
                ins.then_inc(DV.sem[b], 1)

            chain = [("sp", "load", 3), ("pool", "gather", 11), ("pe", "sT", .5), ("act", "sT", .7), ("pe", "k1", 1.2),
                     ("dve", "quad1", .9), ("pe", "sum1", 1.2), ("act", "tanh1", .7), ("pe", "dT", .5), ("act", "dT", .7),
                     ("pe", "k2", 1.2), ("dve", "quad2", .9), ("pe", "sum2", 1.2), ("act", "tanh2", .7), ("dve", "score", .8),
                     ("dve", "leaky", .8), ("act", "exp", .7), ("dve", "weighted", .8), ("dve", "num", 1.4), ("dve", "den", 1.4),
                     ("pe", "den_rows", 0.6), ("dve", "inv_den", 0.25),
                     ("pe", "map", 1.2), ("act", "relu", 1.1), ("dve", "z", .9), ("dve", "stats", 1),
                     ("dve", "moments", .5), ("act", "root", .5), ("dve", "inv", .3), ("dve", "norm", .8),
                     ("pool", "scatter", 7)]
            return Stream(lanes, EG, chain, {"sp": sp_part, "pool": pool_part, "pe": pe_part, "act": act_part,
                                             "dve": dve_part, "free": free}, (PE, AC, DV, LD, IX, GA, SC))

        many = slice(0, 7)
        others = slice(7, 14)
        with ExitStack() as part:
            sweep(chain_stream(part, lanes[many], bank[many], dense=False),
                  slot_of_stream(part, lanes[others]), hist_stream(part, lanes[others], 0, LO_CHUNKS))
        with ExitStack() as part:
            sweep(chain_stream(part, lanes[0:BANKS], bank, dense=True),
                  src_found_stream(part, lanes[BANKS:BANKS + 2]))
        with ExitStack() as part:
            sweep(message_stream(part, lanes[many], bank[many]))

        with ExitStack() as part:
            def tile(name, dt=F32, width=GR):
                return part.enter_context(nc.sbuf_tensor(name, [EG, width], dt))

            found, src_i, end_i, edge_i, row_i = (tile(n, I32) for n in ("found", "src_i2", "end_i", "edge_i2", "row_i"))
            high_i = tile("high_i", I32)
            own, has, pick = tile("own"), tile("has"), tile("pick")
            rec = tile("rec", I32, 4 * GR)
            field = rec[:].rearrange("g (c f) -> g f c", f=4)
            in2, out2 = sem("sources_in"), sem("sources_out")
            block = part.enter_context(nc.Block())

            @block.sync
            def _(sp):
                for t, v in ((found, src_found), (src_i, src_pad), (end_i, sorted_dst_row), (edge_i, edge_id)):
                    sp.dma_start(t[:], block_view(v)).then_inc(in2, 16)
                sp.wait_ge(vectors_ready, 2)
                sp.dma_start(block_view(src_row), row_i[:]).then_inc(out2, 16)
                sp.dma_start(record[0].rearrange("(g c) f -> g (c f)", g=EG), rec[:]).then_inc(out2, 16)
                sp.wait_ge(out2, 32)

            @block.vector
            def _(dve):
                dve.wait_ge(in2, 64)
                nc.vector.tensor_scalar(has[:], found[:], 0.0, None, ALU.is_ge)
                nc.vector.tensor_scalar(high_i[:], src_i[:], LO.bit_length() - 1, None, ALU.logical_shift_right)
                link(dve, nc.vector.tensor_scalar(own[:], edge_i[:], float(EP), None, ALU.add))
                link(dve, nc.vector.tensor_tensor(pick[:], found[:], own[:], ALU.subtract))
                link(dve, nc.vector.tensor_tensor(pick[:], pick[:], has[:], ALU.mult))
                link(dve, nc.vector.tensor_tensor(row_i[:], pick[:], own[:], ALU.add))
                nc.vector.tensor_copy(field[:, 0, :], high_i[:])
                nc.vector.tensor_copy(field[:, 1, :], src_i[:])
                nc.vector.tensor_copy(field[:, 2, :], row_i[:])
                nc.vector.tensor_copy(field[:, 3, :], end_i[:]).then_inc(vectors_ready, 1)


        bin_bases(0, LO_CHUNKS)
        with ExitStack() as part:
            sweep(edge_stream(part, lanes[many], bank[many], 1), rank_stream(part, lanes[others], 0, LO_CHUNKS, spare))

        with ExitStack() as part:
            rec = part.enter_context(nc.sbuf_tensor("rec1", [EG, 4 * GR], I32))
            high = part.enter_context(nc.sbuf_tensor("high", [EG, GR], F32))
            in3, out3, high_ready = sem("rec1_in"), sem("high_out"), sem("high_ready")
            block = part.enter_context(nc.Block())

            @block.sync
            def _(sp):
                sp.dma_start(rec[:], record[1].rearrange("(g c) f -> g (c f)", g=EG)).then_inc(in3, 16)
                sp.wait_ge(high_ready, 1)
                sp.dma_start(block_view(digit[1]), high[:]).then_inc(out3, 16)
                sp.wait_ge(out3, 16)

            @block.vector
            def _(dve):
                dve.wait_ge(in3, 16)
                nc.vector.tensor_copy(high[:], rec[:].rearrange("g (c f) -> g f c", f=4)[:, 0, :]).then_inc(high_ready, 1)


        with ExitStack() as part:
            sweep(edge_stream(part, lanes[many], bank[many], 2), hist_stream(part, lanes[others], 1, HI_CHUNKS))
        bin_bases(1, HI_CHUNKS)
        with ExitStack() as part:
            sweep(edge_stream(part, lanes[many], bank[many], 3), rank_stream(part, lanes[others], 1, HI_CHUNKS, spare))

        with ExitStack() as part:
            def tile(name, dt=F32, width=GR):
                return part.enter_context(nc.sbuf_tensor(name, [EG, width], dt))

            rec = tile("rec2", I32, 4 * GR)
            src_s, prev_s, next_s, row_s, end_s, out_s = (tile(n, I32) for n in
                                                          ("src_s", "prev_s", "next_s", "row_s", "end_s", "out_s"))
            mask, end, tmp, tmp2 = (tile(n) for n in ("mask_s", "end_flag_s", "tmp_s", "tmp2_s"))
            in4, out4, fields, around, done4 = (sem(n) for n in ("rec2_in", "sorted_out", "fields", "around", "sorted_done"))
            field = rec[:].rearrange("g (c f) -> g f c", f=4)
            block = part.enter_context(nc.Block())

            @block.sync
            def _(sp):
                sp.dma_start(rec[:], record[2].rearrange("(g c) f -> g (c f)", g=EG)).then_inc(in4, 16)
                sp.wait_ge(fields, 1)
                sp.dma_start(block_view(sorted_src, 1), src_s[:]).then_inc(out4, 16)
                sp.dma_start(block_view(sorted_src_row), row_s[:]).then_inc(out4, 16)
                sp.dma_start(block_view(sorted_dst_row), end_s[:]).then_inc(out4, 16)
                sp.wait_ge(out4, 48)
                sp.dma_start(prev_s[:], block_view(sorted_src, 0)).then_inc(around, 16)
                sp.dma_start(next_s[:], block_view(sorted_src, 2)).then_inc(around, 16)
                sp.wait_ge(done4, 1)
                sp.dma_start(block_view(sorted_mask), mask[:]).then_inc(out4, 16)
                sp.dma_start(block_view(src_out_idx), out_s[:]).then_inc(out4, 16)
                sp.wait_ge(out4, 80)

            @block.vector
            def _(dve):
                dve.wait_ge(in4, 16)
                nc.vector.tensor_copy(src_s[:], field[:, 1, :])
                nc.vector.tensor_copy(row_s[:], field[:, 2, :])
                nc.vector.tensor_copy(end_s[:], field[:, 3, :]).then_inc(fields, 1)
                dve.wait_ge(around, 32)
                nc.vector.tensor_tensor(mask[:], src_s[:], prev_s[:], ALU.is_equal)
                nc.vector.tensor_tensor(end[:], src_s[:], next_s[:], ALU.not_equal)
                nc.vector.tensor_scalar(tmp[:], src_s[:], float(-OOB), None, ALU.add)
                link(dve, nc.vector.tensor_scalar(tmp2[:], src_s[:], float(N), None, ALU.is_lt))
                link(dve, nc.vector.tensor_tensor(tmp2[:], tmp2[:], end[:], ALU.mult))
                link(dve, nc.vector.tensor_tensor(tmp[:], tmp[:], tmp2[:], ALU.mult))
                nc.vector.tensor_scalar(out_s[:], tmp[:], float(OOB), None, ALU.add).then_inc(done4, 1)


        with ExitStack() as part:
            sweep(edge_stream(part, lanes[many], bank[many], 4))

        with ExitStack() as part:
            mean, square, var = (part.enter_context(nc.sbuf_tensor(n, [P, 1], F32)) for n in ("bn_mean", "bn_square", "bn_var"))
            var_ready, root_ready = sem("var_ready"), sem("bn_root")
            block = part.enter_context(nc.Block())

            @block.vector
            def _(dve):
                for t in bn_part:
                    link(dve, nc.vector.tensor_tensor(bn_sum[:], bn_sum[:], t[:], ALU.add))
                nc.vector.tensor_scalar(mean[:], bn_sum[:, 0:1], 1.0 / N, None, ALU.mult)
                link(dve, nc.vector.tensor_scalar(var[:], bn_sum[:, 1:2], 1.0 / N, None, ALU.mult))
                link(dve, nc.vector.tensor_tensor(square[:], mean[:], mean[:], ALU.mult))
                nc.vector.tensor_tensor(var[:], var[:], square[:], ALU.subtract).then_inc(var_ready, 1)
                dve.wait_ge(root_ready, 1)
                link(dve, nc.vector.reciprocal(var[:], var[:]))
                link(dve, nc.vector.tensor_tensor(bn_a[:], colb["gamma"][:], var[:], ALU.mult))
                link(dve, nc.vector.tensor_tensor(square[:], mean[:], bn_a[:], ALU.mult))
                link(dve, nc.vector.tensor_tensor(bn_c[:], colb["beta"][:], square[:], ALU.subtract))

            @block.scalar
            def _(act):
                act.wait_ge(var_ready, 1)
                nc.scalar.activation(var[:], var[:], ACT.Sqrt, bias=eps[:]).then_inc(root_ready, 1)

        with ExitStack() as part:
            sweep(attention_stream(part, lanes[many], bank[many]))


_INS = ["x", "src", "dst", "edge_attr_128", "edge_weight",
        "L0_gnn_W1", "L0_gnn_b1", "L0_gnn_W2", "L0_gnn_b2", "L0_gnn_U1", "L0_gnn_ub1", "L0_gnn_U2", "L0_gnn_ub2",
        "L0_gnn_ln_w", "L0_gnn_ln_b",
        "L1_gnn_W1_l", "L1_gnn_b1", "L1_gnn_W1_r", "L1_gnn_W2_l", "L1_gnn_b2", "L1_gnn_W2_r",
        "L2_gnn_W1", "L2_gnn_b1", "L2_gnn_W2", "L2_gnn_b2",
        "L3_gnn_kernel", "L3_gnn_kernel1", "L3_gnn_kernel2", "L3_gnn_gamma", "L3_gnn_beta"]


def program(nc, a, out):
    w1, u1 = a["L0_gnn_W1"], a["L0_gnn_U1"]
    w = {
        "matrices": {
            "msg_src": w1[0:D, :], "msg_dst": w1[D:2 * D, :], "msg_edge": w1[2 * D:3 * D, :], "msg_out": a["L0_gnn_W2"],
            "upd_x": u1[0:D, :], "upd_agg": u1[D:2 * D, :], "upd_out": a["L0_gnn_U2"],
            "sage1_l": a["L1_gnn_W1_l"], "sage1_r": a["L1_gnn_W1_r"],
            "sage2_l": a["L1_gnn_W2_l"], "sage2_r": a["L1_gnn_W2_r"],
            "gcn1": a["L2_gnn_W1"], "gcn2": a["L2_gnn_W2"],
            "map": a["L3_gnn_kernel"], "k1": a["L3_gnn_kernel1"], "k2": a["L3_gnn_kernel2"]},
        "columns": {"msg_b1": a["L0_gnn_b1"], "msg_b2": a["L0_gnn_b2"], "upd_b1": a["L0_gnn_ub1"],
                    "sage_b1": a["L1_gnn_b1"], "gcn_b1": a["L2_gnn_b1"],
                    "gamma": a["L3_gnn_gamma"], "beta": a["L3_gnn_beta"]},
        "rows": {"upd_b2": a["L0_gnn_ub2"], "sage_b2": a["L1_gnn_b2"], "gcn_b2": a["L2_gnn_b2"]},
        "ln_w": a["L0_gnn_ln_w"], "ln_b": a["L0_gnn_ln_b"],
    }
    build(nc, a["x"], a["src"], a["dst"], a["edge_attr_128"], a["edge_weight"], w, out)


def kernel(**inputs):
    import numpy as _np
    import concourse.bacc as _bacc
    from concourse import mybir as _mybir
    from concourse.bass_utils import run_bass_kernel_spmd as _run

    nc = _bacc.Bacc("TRN2", target_bir_lowering=False, num_devices=1)
    arrays, args = {}, {}
    for name in _INS:
        a = _np.ascontiguousarray(inputs[name])
        arrays[f"in_{name}_dram"] = a
        args[name] = nc.dram_tensor(f"in_{name}_dram", a.shape, _mybir.dt.from_np(a.dtype), kind="ExternalInput").ap()
    out = nc.dram_tensor("out_0_dram", inputs["x"].shape, _mybir.dt.float32, kind="ExternalOutput").ap()
    program(nc, args, out)
    r = _run(nc, [arrays], core_ids=[0])
    return r.results[0]["out_0_dram"]
```
